# Optimizing a Trainium2 kernel written in Bass

```python
import numpy as np
import jax
import jax.numpy as jnp

def _softmax(x, axis=-1):
    return jax.nn.softmax(x, axis=axis)

def _gelu(x):
    return jax.nn.gelu(x, approximate=True)

def _silu(x):
    return jax.nn.silu(x)

def _sigmoid(x):
    return jax.nn.sigmoid(x)

def _layernorm(x, axis=-1, eps=1e-05):
    m = jnp.mean(x, axis=axis, keepdims=True)
    v = jnp.var(x, axis=axis, keepdims=True)
    return (x - m) / jnp.sqrt(v + eps)

def _scatter_add(tgt, idx, src, axis=0):
    return tgt.at[idx].add(src)

def _segment_sum(src, seg, n):
    return jax.ops.segment_sum(src, seg, n)
kernel_name = 'mk_gnn_resnorm_d2_gnn_r8_874582'

def setup_inputs(seed: int=0):
    np.random.seed(seed)
    _w = jnp.asarray

    def _rec_inputs():
        import jax
        import jax.numpy as jnp
        _gk = jax.random.key(seed)
        x = -0.0002117 + 1 * jax.random.normal(jax.random.fold_in(_gk, 1), (6250, 512), jnp.float32)
        src = jax.random.randint(jax.random.fold_in(_gk, 2), (100000,), 0, 6250, jnp.int32)
        dst = jnp.minimum((6250 * jax.random.uniform(jax.random.fold_in(_gk, 3), (100000,)) ** 2.0).astype(jnp.int32), 49999)
        _o = jnp.argsort(dst, stable=True)
        src = src[_o]
        dst = dst[_o]
        edge_attr_4 = 0.00171547 + 0.999346 * jax.random.normal(jax.random.fold_in(_gk, 12), (100000, 4), jnp.float32)
        edge_attr_8 = 0.000126197 + 0.999763 * jax.random.normal(jax.random.fold_in(_gk, 13), (100000, 8), jnp.float32)
        return (x, src, dst, edge_attr_4, edge_attr_8)
    x, src, dst, edge_attr_4, edge_attr_8 = _rec_inputs()

    def _L0_gnn_setup():
        import jax, jax.numpy as jnp
        import numpy as np
        N = 6250
        E = 50000
        D_IN = 512
        D_OUT = 512
        LN_EPS = 1e-05
        key = jax.random.key(seed)
        ks = jax.random.split(key, 8)
        x = jax.random.normal(ks[0], (N, D_IN), dtype=jnp.float32)
        src = jax.random.randint(ks[1], (E,), 0, N, dtype=jnp.int32)
        dst = jnp.sort(jax.random.randint(ks[2], (E,), 0, N, dtype=jnp.int32))
        bound = 1.0 / np.sqrt(D_IN)
        W_self = jax.random.uniform(ks[3], (D_IN, D_OUT), minval=-bound, maxval=bound, dtype=jnp.float32)
        b_self = jax.random.uniform(ks[4], (D_OUT,), minval=-bound, maxval=bound, dtype=jnp.float32)
        W_neigh = jax.random.uniform(ks[5], (D_IN, D_OUT), minval=-bound, maxval=bound, dtype=jnp.float32)
        gamma = jnp.ones((D_OUT,), dtype=jnp.float32)
        beta = jnp.zeros((D_OUT,), dtype=jnp.float32)
        alpha = jnp.array(0.25, dtype=jnp.float32)
        return {'x': x, 'src': src, 'dst': dst, 'W_self': W_self, 'b_self': b_self, 'W_neigh': W_neigh, 'gamma': gamma, 'beta': beta, 'alpha': alpha}
    _L0_gnn_all = _L0_gnn_setup()
    _L0_gnn_in = {k: v for k, v in _L0_gnn_all.items() if k in ('W_self', 'b_self', 'W_neigh', 'gamma', 'beta', 'alpha')}
    del _L0_gnn_all

    def _L1_gnn_setup():
        import jax, jax.numpy as jnp
        import numpy as np
        MUL = 128
        N_NODES = 1250
        N_EDGES = 20000
        R_BASIS = 8
        HIDDEN = 64
        W_NUMEL = 4 * MUL
        SQRT3 = 3.0 ** 0.5
        SILU_2MOM = 1.679177
        AVG_NUM_NEIGHBORS = 10.0

        def _lin_irreps(x0, x1, W0, W1):
            y0 = x0 @ W0 / jnp.sqrt(jnp.float32(W0.shape[0]))
            y1 = jnp.einsum('num,uv->nvm', x1, W1) / jnp.sqrt(jnp.float32(W1.shape[0]))
            return (y0, y1)

        def _forward(node_feats, edge_attrs, edge_feats, edge_index, W_up0, W_up1, W_mlp1, W_mlp2, W_mlp3, W_mlp4, W_out0, W_out1):
            num_nodes = node_feats.shape[0]
            sender, receiver = (edge_index[0], edge_index[1])
            x0 = node_feats[:, :MUL]
            x1 = node_feats[:, MUL:].reshape(num_nodes, MUL, 3)
            x0, x1 = _lin_irreps(x0, x1, W_up0, W_up1)
            h = edge_feats
            for W in (W_mlp1, W_mlp2, W_mlp3):
                h = SILU_2MOM * jax.nn.silu(h @ W / jnp.sqrt(jnp.float32(W.shape[0])))
            tpw = h @ W_mlp4 / jnp.sqrt(jnp.float32(W_mlp4.shape[0]))
            w1, w2, w3, w4 = jnp.split(tpw, 4, axis=-1)
            s0 = x0[sender]
            s1 = x1[sender]
            y0 = edge_attrs[:, 0:1]
            y1 = edge_attrs[:, 1:4]
            p1 = w1 * s0 * y0
            p2 = (w2 * s0)[:, :, None] * y1[:, None, :]
            p3 = w3[:, :, None] * s1 * y0[:, None, :]
            p4 = w4 * jnp.einsum('eum,em->eu', s1, y1) / SQRT3
            m0 = jnp.concatenate([p1, p4], axis=-1)
            m1 = jnp.concatenate([p2, p3], axis=1)
            msg0 = jax.ops.segment_sum(m0, receiver, num_segments=num_nodes)
            msg1 = jax.ops.segment_sum(m1, receiver, num_segments=num_nodes)
            o0, o1 = _lin_irreps(msg0, msg1, W_out0, W_out1)
            out = jnp.concatenate([o0, o1.reshape(num_nodes, 3 * MUL)], axis=-1)
            return out / AVG_NUM_NEIGHBORS
        key = jax.random.key(seed)
        ks = jax.random.split(key, 12)
        rn = lambda k, s: jax.random.normal(k, s, dtype=jnp.float32)
        return {'node_feats': rn(ks[0], (N_NODES, 4 * MUL)), 'edge_attrs': rn(ks[1], (N_EDGES, 4)), 'edge_feats': rn(ks[2], (N_EDGES, R_BASIS)), 'edge_index': jax.random.randint(ks[3], (2, N_EDGES), 0, N_NODES), 'W_up0': rn(ks[4], (MUL, MUL)), 'W_up1': rn(ks[5], (MUL, MUL)), 'W_mlp1': rn(ks[6], (R_BASIS, HIDDEN)), 'W_mlp2': rn(ks[7], (HIDDEN, HIDDEN)), 'W_mlp3': rn(ks[8], (HIDDEN, HIDDEN)), 'W_mlp4': rn(ks[9], (HIDDEN, W_NUMEL)), 'W_out0': rn(ks[10], (2 * MUL, MUL)), 'W_out1': rn(ks[11], (2 * MUL, MUL))}
    _L1_gnn_all = _L1_gnn_setup()
    _L1_gnn_in = {k: v for k, v in _L1_gnn_all.items() if k in ('W_up0', 'W_up1', 'W_mlp1', 'W_mlp2', 'W_mlp3', 'W_mlp4', 'W_out0', 'W_out1')}
    del _L1_gnn_all
    return {'x': x, 'src': src, 'dst': dst, 'edge_attr_4': edge_attr_4, 'edge_attr_8': edge_attr_8, 'L0_gnn_W_self': _L0_gnn_in['W_self'], 'L0_gnn_b_self': _L0_gnn_in['b_self'], 'L0_gnn_W_neigh': _L0_gnn_in['W_neigh'], 'L0_gnn_gamma': _L0_gnn_in['gamma'], 'L0_gnn_beta': _L0_gnn_in['beta'], 'L0_gnn_alpha': _L0_gnn_in['alpha'], 'L1_gnn_W_up0': _L1_gnn_in['W_up0'], 'L1_gnn_W_up1': _L1_gnn_in['W_up1'], 'L1_gnn_W_mlp1': _L1_gnn_in['W_mlp1'], 'L1_gnn_W_mlp2': _L1_gnn_in['W_mlp2'], 'L1_gnn_W_mlp3': _L1_gnn_in['W_mlp3'], 'L1_gnn_W_mlp4': _L1_gnn_in['W_mlp4'], 'L1_gnn_W_out0': _L1_gnn_in['W_out0'], 'L1_gnn_W_out1': _L1_gnn_in['W_out1']}

def reference(x, src, dst, edge_attr_4, edge_attr_8, L0_gnn_W_self, L0_gnn_b_self, L0_gnn_W_neigh, L0_gnn_gamma, L0_gnn_beta, L0_gnn_alpha, L1_gnn_W_up0, L1_gnn_W_up1, L1_gnn_W_mlp1, L1_gnn_W_mlp2, L1_gnn_W_mlp3, L1_gnn_W_mlp4, L1_gnn_W_out0, L1_gnn_W_out1):
    import jax
    import jax.numpy as jnp

    def _L0_gnn_ref(x, src, dst, W_self, b_self, W_neigh, gamma, beta, alpha):
        import jax, jax.numpy as jnp
        import numpy as np
        N = 6250
        E = 50000
        D_IN = 512
        D_OUT = 512
        LN_EPS = 1e-05
        deg = jax.ops.segment_sum(jnp.ones_like(src, dtype=x.dtype), dst, num_segments=N)
        inv_deg = 1.0 / jnp.maximum(deg, 1.0)
        agg = jax.ops.segment_sum(x[src], dst, num_segments=N)
        neigh = agg * inv_deg[:, None]
        h = x @ W_self + b_self + neigh @ W_neigh
        mu = jnp.mean(h, axis=-1, keepdims=True)
        var = jnp.mean(jnp.square(h - mu), axis=-1, keepdims=True)
        h = (h - mu) * jax.lax.rsqrt(var + LN_EPS) * gamma + beta
        h = jnp.where(h >= 0, h, alpha * h)
        return h + x

    def _L1_gnn_ref(node_feats, edge_attrs, edge_feats, edge_index, W_up0, W_up1, W_mlp1, W_mlp2, W_mlp3, W_mlp4, W_out0, W_out1):
        import jax, jax.numpy as jnp
        import numpy as np
        MUL = 128
        N_NODES = 1250
        N_EDGES = 20000
        R_BASIS = 8
        HIDDEN = 64
        W_NUMEL = 4 * MUL
        SQRT3 = 3.0 ** 0.5
        SILU_2MOM = 1.679177
        AVG_NUM_NEIGHBORS = 10.0

        def _lin_irreps(x0, x1, W0, W1):
            y0 = x0 @ W0 / jnp.sqrt(jnp.float32(W0.shape[0]))
            y1 = jnp.einsum('num,uv->nvm', x1, W1) / jnp.sqrt(jnp.float32(W1.shape[0]))
            return (y0, y1)

        def _forward(node_feats, edge_attrs, edge_feats, edge_index, W_up0, W_up1, W_mlp1, W_mlp2, W_mlp3, W_mlp4, W_out0, W_out1):
            num_nodes = node_feats.shape[0]
            sender, receiver = (edge_index[0], edge_index[1])
            x0 = node_feats[:, :MUL]
            x1 = node_feats[:, MUL:].reshape(num_nodes, MUL, 3)
            x0, x1 = _lin_irreps(x0, x1, W_up0, W_up1)
            h = edge_feats
            for W in (W_mlp1, W_mlp2, W_mlp3):
                h = SILU_2MOM * jax.nn.silu(h @ W / jnp.sqrt(jnp.float32(W.shape[0])))
            tpw = h @ W_mlp4 / jnp.sqrt(jnp.float32(W_mlp4.shape[0]))
            w1, w2, w3, w4 = jnp.split(tpw, 4, axis=-1)
            s0 = x0[sender]
            s1 = x1[sender]
            y0 = edge_attrs[:, 0:1]
            y1 = edge_attrs[:, 1:4]
            p1 = w1 * s0 * y0
            p2 = (w2 * s0)[:, :, None] * y1[:, None, :]
            p3 = w3[:, :, None] * s1 * y0[:, None, :]
            p4 = w4 * jnp.einsum('eum,em->eu', s1, y1) / SQRT3
            m0 = jnp.concatenate([p1, p4], axis=-1)
            m1 = jnp.concatenate([p2, p3], axis=1)
            msg0 = jax.ops.segment_sum(m0, receiver, num_segments=num_nodes)
            msg1 = jax.ops.segment_sum(m1, receiver, num_segments=num_nodes)
            o0, o1 = _lin_irreps(msg0, msg1, W_out0, W_out1)
            out = jnp.concatenate([o0, o1.reshape(num_nodes, 3 * MUL)], axis=-1)
            return out / AVG_NUM_NEIGHBORS
        return _forward(node_feats, edge_attrs, edge_feats, edge_index, W_up0, W_up1, W_mlp1, W_mlp2, W_mlp3, W_mlp4, W_out0, W_out1)
    edge_index = jnp.stack([src, dst])
    x = _layernorm(x + _L0_gnn_ref(x, src, dst, L0_gnn_W_self, L0_gnn_b_self, L0_gnn_W_neigh, L0_gnn_gamma, L0_gnn_beta, L0_gnn_alpha), axis=-1)
    x = _layernorm(x + _L1_gnn_ref(x, edge_attr_4, edge_attr_8, edge_index, L1_gnn_W_up0, L1_gnn_W_up1, L1_gnn_W_mlp1, L1_gnn_W_mlp2, L1_gnn_W_mlp3, L1_gnn_W_mlp4, L1_gnn_W_out0, L1_gnn_W_out1), axis=-1)
    return x

_drawn_inputs = setup_inputs


def setup_inputs(seed=0):
    import zlib

    import numpy as np

    out = dict(_drawn_inputs(seed))
    spreads = {'L0_gnn_gamma': (1.0, 0.2), 'L0_gnn_beta': (0.0, 0.1)}
    factors = {'L0_gnn_b_self': 3.92}
    for name, (base, spread) in spreads.items():
        noise = np.random.default_rng([zlib.crc32(name.encode()), seed]).standard_normal(out[name].shape)
        drawn = base * np.exp(spread * noise) if base else spread * noise
        out[name] = jnp.asarray(drawn.astype(out[name].dtype))
    for name, factor in factors.items():
        out[name] = (out[name] * factor).astype(out[name].dtype)
    return out
```

```python
import math
from contextlib import ExitStack

import concourse.bass as bass
from concourse import mybir

N = 6250
E = 100000
D = 512
P = 128
MUL = 128
HID = 64
RB = 8
BLK = 8
BODY = 2 * BLK
T = -(-E // (P * BODY)) * BODY
LOOPS = T // BODY
NBLK = T // BLK
NT = -(-N // P)
NPAD = (NT + 1) * P
NODE_LOOPS = (NT - 1) // 2
AR = 4
SKIP = 8191.0
LN_EPS = 1e-5
SILU_2MOM = 1.679177
AVG_NEIGHBORS = 10.0
CREDIT = 4

fp32 = mybir.dt.float32
i32 = mybir.dt.int32
ALU = mybir.AluOpType
ACT = mybir.ActivationFunctionType


def after(k):
    return k + (CREDIT + 1)


def build(nc, x, src, dst, dst_before, dst_after, edge_y, edge_feats, w_self, b_self, w_neigh,
          gamma, beta, alpha, w_up0, w_up1, w_mlp1, w_mlp2, w_mlp3, w_mlp4, w_out0, w_out1, out):
    ctx = ExitStack()
    with ctx:
        def sb(name, shape, dt=fp32):
            return ctx.enter_context(nc.sbuf_tensor(name, shape, dt))

        def sem(name):
            return ctx.enter_context(nc.semaphore(name))

        def sems(name, n):
            return [sem(f"{name}{k}") for k in range(n)]

        agg_dram = nc.dram_tensor("agg_dram", [NPAD, D + 1], fp32, kind="Internal").ap()
        x1_dram = nc.dram_tensor("x1_dram", [NPAD, D], fp32, kind="Internal").ap()
        up_dram = nc.dram_tensor("up_dram", [NPAD, D], fp32, kind="Internal").ap()
        msg_dram = nc.dram_tensor("msg_dram", [NPAD, 2 * D], fp32, kind="Internal").ap()

        column_no = sb("column_no", [P, P])
        identity = sb("identity", [P, P])
        upto = sb("upto", [P, P])
        ones = sb("ones", [P, P])
        zeros = sb("zeros", [P, 2 * D])
        dst_sb = sb("dst_sb", [P, T], i32)
        before_sb = sb("before_sb", [P, T], i32)
        after_sb = sb("after_sb", [P, T], i32)
        opens = sb("opens", [P, T])
        closes = sb("closes", [P, T])
        runs = sb("runs", [P, T])
        run_sum = sb("run_sum", [P, T])
        all_one = sb("all_one", [P, T])
        all_sum = sb("all_sum", [P, T])
        run_int = sb("run_int", [P, T], i32)
        meta = sb("meta", [P, T + BLK, 4])
        y_sb = sb("y_sb", [P, T + BLK, 4])
        meta_blk = sb("meta_blk", [P, 2, BLK, 4])
        y_blk = sb("y_blk", [P, 2, BLK, 4])
        src_blk = sb("src_blk", [P, 2, BLK], i32)
        rows = sb("rows", [P, BLK, D])
        pick = sb("pick", [P, 2, P])
        pick_y = sb("pick_y", [P, 2, 4, P])
        side = sb("side", [P, AR, 3])
        row_index = sb("row_index", [P, AR], i32)
        acc = sb("acc", [P, AR, 2 * D])
        msg = sb("msg", [P, 2, 6, MUL])
        dot0 = sb("dot0", [P, 2, MUL])
        dot1 = sb("dot1", [P, MUL])
        dot2 = sb("dot2", [P, MUL])
        feats = sb("feats", [2 * RB, 2, 512])
        hid1 = sb("hid1", [P, 512])
        hid2 = sb("hid2", [P, 512])
        hid3 = sb("hid3", [P, 2, 512])
        ws_sb = sb("ws_sb", [P, 4, D])
        wn_sb = sb("wn_sb", [P, 4, D])
        wup_sb = sb("wup_sb", [P, 2, MUL])
        w1_sb = sb("w1_sb", [2 * RB, P])
        w2_sb = sb("w2_sb", [P, P])
        w3_sb = sb("w3_sb", [P, P])
        w4_raw = sb("w4_raw", [P, D])
        w4_sb = sb("w4_sb", [P, D])
        wout_sb = sb("wout_sb", [P, 4, MUL])
        bias_sb = sb("bias_sb", [P, D])
        gamma_sb = sb("gamma_sb", [P, D])
        beta_sb = sb("beta_sb", [P, D])
        alpha_sb = sb("alpha_sb", [P, 1])
        eps_sb = sb("eps_sb", [P, 1])
        nx = sb("nx", [P, 2, D])
        nagg = sb("nagg", [P, 2, D + 1])
        nneigh = sb("nneigh", [P, 2, D])
        nh = sb("nh", [P, D])
        nhn = sb("nhn", [P, D])
        nhg = sb("nhg", [P, D])
        nhb = sb("nhb", [P, D])
        nlow = sb("nlow", [P, D])
        nact = sb("nact", [P, D])
        nres = sb("nres", [P, D])
        nout = sb("nout", [P, 2, D])
        nup = sb("nup", [P, 2, D])
        stats = sb("stats", [P, 6])
        mv = sb("mv", [P, 2])
        std = sb("std", [P, 1])
        rstd = sb("rstd", [P, 1])
        shift = sb("shift", [P, 1])
        cnt = sb("cnt", [P, 1])
        inv = sb("inv", [P, 1])

        bank = [ctx.enter_context(nc.psum_tensor(f"bank{k}", [P, 512], fp32)) for k in range(8)]

        gate = sems("gate", 2)
        p_tab = sem("p_tab")
        p_wts = sem("p_wts")
        p_w2 = sem("p_w2")
        p_zero = sem("p_zero")
        p_pad = sem("p_pad")
        p_fill = sem("p_fill")
        p_chain = sem("p_chain")
        p_runs = sem("p_runs")
        p_meta = sem("p_meta")
        p_w4 = sem("p_w4")
        e_src = [sems(f"e{l}_src", 2) for l in range(2)]
        e_meta = [sem(f"e{l}_meta") for l in range(2)]
        e_row = [sems(f"e{l}_row", BLK) for l in range(2)]
        e_pick = [sem(f"e{l}_pick") for l in range(2)]
        e_sidep = [sem(f"e{l}_sidep") for l in range(2)]
        e_side = [sem(f"e{l}_side") for l in range(2)]
        e_sum = [sem(f"e{l}_sum") for l in range(2)]
        e_acc = [sem(f"e{l}_acc") for l in range(2)]
        e_idx = [sem(f"e{l}_idx") for l in range(2)]
        e_out = [sems(f"e{l}_out", AR) for l in range(2)]
        m_feat = sems("m_feat", 2)
        m_z = sem("m_z")
        m_h = sem("m_h")
        m_tpw = sem("m_tpw")
        m_picky = sem("m_picky")
        m_dot0 = sem("m_dot0")
        m_dot = sem("m_dot")
        m_msg = sem("m_msg")
        n_in = [sems(f"n{l}_in", 2) for l in range(2)]
        n_neigh = sem("n_neigh")
        n_pre = sem("n_pre")
        n_chain = [sem(f"n{l}_chain") for l in range(2)]
        n_tp = [sem(f"n{l}_tp") for l in range(2)]
        n_te = [sem(f"n{l}_te") for l in range(2)]
        n_te2 = sem("n_te2")
        n_h = [sem(f"n{l}_h") for l in range(2)]
        n_hread = sem("n_hread")
        n_var = [sem(f"n{l}_var") for l in range(2)]
        n_std = [sem(f"n{l}_std") for l in range(2)]
        n_shift = [sem(f"n{l}_shift") for l in range(2)]
        n_norm = sem("n_norm")
        n_gm = sem("n_gm")
        n_gb = sem("n_gb")
        n_res = [sem(f"n{l}_res") for l in range(2)]
        n_fin = [sem(f"n{l}_fin") for l in range(2)]
        n_x1t = sem("n_x1t")
        n_x1e = sem("n_x1e")
        n_upp = sem("n_upp")
        n_up = sem("n_up")
        n_st = [sem(f"n{l}_st") for l in range(2)]
        n_stored = [sem(f"n{l}_stored") for l in range(2)]

        block = ctx.enter_context(nc.Block())

        def passed(eng):
            eng.sem_inc(gate[0] if eng is nc.gpsimd else gate[1], 1)

        @block.sync
        def _(sp):
            for s in n_stored:
                sp.sem_inc(s, CREDIT)
            sp.dma_start(dst_sb[:, :], dst).then_inc(p_tab, 16)
            sp.dma_start(before_sb[:, :], dst_before).then_inc(p_tab, 16)
            sp.dma_start(after_sb[:, :], dst_after).then_inc(p_tab, 16)

            def index_block(l, b, h):
                sp.dma_start(src_blk[:, h, :], src[:, bass.ds(b * BLK, BLK)]).then_inc(e_src[l][h], 16)

            index_block(0, 0, 0)
            index_block(0, 1, 1)
            sp.dma_start(y_sb[:, :, :], edge_y).then_inc(p_wts, 16)
            sp.dma_start(ws_sb[:, :, :], w_self.rearrange("(c p) n -> p c n", p=P)).then_inc(p_wts, 16)
            sp.dma_start(wn_sb[:, :, :], w_neigh.rearrange("(c p) n -> p c n", p=P)).then_inc(p_wts, 16)
            sp.dma_start(wup_sb[:, 0, :], w_up0).then_inc(p_wts, 16)
            sp.dma_start(wup_sb[:, 1, :], w_up1).then_inc(p_wts, 16)
            sp.dma_start(wout_sb[:, 0:2, :], w_out0.rearrange("(c p) n -> p c n", p=P)).then_inc(p_wts, 16)
            sp.dma_start(wout_sb[:, 2:4, :], w_out1.rearrange("(c p) n -> p c n", p=P)).then_inc(p_wts, 16)
            sp.dma_start(bias_sb[:, :], b_self.to_broadcast([P, D])).then_inc(p_wts, 16)
            sp.dma_start(gamma_sb[:, :], gamma.to_broadcast([P, D])).then_inc(p_wts, 16)
            sp.dma_start(beta_sb[:, :], beta.to_broadcast([P, D])).then_inc(p_wts, 16)
            sp.dma_start(alpha_sb[:, :], alpha.to_broadcast([P, 1])).then_inc(p_wts, 16)
            sp.dma_start(w4_raw[0:HID, :], w_mlp4).then_inc(p_w2, 16)
            sp.dma_start(w4_raw[HID:P, :], w_mlp4).then_inc(p_w2, 16)
            sp.wait_ge(p_fill, 2)
            for k in range(2):
                sp.dma_start(w1_sb[k * RB:(k + 1) * RB, k * HID:(k + 1) * HID], w_mlp1).then_inc(p_w2, 16)
                sp.dma_start(w2_sb[k * HID:(k + 1) * HID, k * HID:(k + 1) * HID], w_mlp2).then_inc(p_w2, 16)
                sp.dma_start(w3_sb[k * HID:(k + 1) * HID, k * HID:(k + 1) * HID], w_mlp3).then_inc(p_w2, 16)

            def index_loop(l):
                with sp.Fori(0, LOOPS) as i:
                    for h in range(2):
                        b = i * 2 + h
                        if l == 1:
                            sp.wait_ge(m_z, b * 3 + 1)
                            load_feats(b + 2, h)
                        for r in range(BLK):
                            sp.wait_ge(e_row[l][r], (b + 1) * 16)
                        index_block(l, b + 2, h)

            def load_feats(b, h):
                sp.dma_start(feats[:, h, :], edge_feats[:, bass.ds(b * 512, 512)]).then_inc(m_feat[h], 16)

            def edges_done(l):
                for r in range(BLK):
                    sp.wait_ge(e_row[l][r], 16 * (NBLK + 1))
                for r in range(AR):
                    sp.wait_ge(e_out[l][r], 16 * (T // AR + 1))

            index_loop(0)
            edges_done(0)

            def node0_in(n, r):
                sp.dma_start(nx[:, r, :], x[bass.ds(n * P, P), :]).then_inc(n_in[0][r], 16)
                sp.dma_start(nagg[:, r, :], agg_dram[bass.ds(n * P, P), :]).then_inc(n_in[0][r], 16)

            def node0_out(n, r):
                sp.wait_ge(n_fin[0], after(n))
                sp.dma_start(x1_dram[bass.ds(n * P, P), :], nout[:, r, :]).then_inc(n_st[0], 16)
                sp.wait_ge(n_up, after(n))
                sp.dma_start(up_dram[bass.ds(n * P, P), :], nup[:, r, :]).then_inc(n_st[0], 16)
                sp.wait_ge(n_st[0], (n + 1) * 32)
                sp.sem_inc(n_stored[0], 1)

            node0_in(0, 0)
            node0_in(1, 1)
            with sp.Fori(0, NODE_LOOPS) as i:
                for r in range(2):
                    n = i * 2 + r
                    sp.wait_ge(n_res[0], after(n))
                    node0_in(n + 2, r)
                    node0_out(n, r)
            node0_out(NT - 1, 0)
            sp.wait_ge(n_in[0][1], 32 * (NODE_LOOPS + 1))

            index_block(1, 0, 0)
            index_block(1, 1, 1)
            load_feats(0, 0)
            load_feats(1, 1)
            index_loop(1)
            edges_done(1)

            def node1_in(n, r):
                sp.dma_start(nx[:, r, :], x1_dram[bass.ds(n * P, P), :]).then_inc(n_in[1][r], 16)
                sp.dma_start(acc[:, r, :], msg_dram[bass.ds(n * P, P), :]).then_inc(n_in[1][r], 16)

            def node1_out(n, r):
                sp.wait_ge(n_fin[1], after(n))
                sp.dma_start(out[bass.ds(n * P, P), :], nout[:, r, :]).then_inc(n_st[1], 16)
                sp.wait_ge(n_st[1], (n + 1) * 16)
                sp.sem_inc(n_stored[1], 1)

            sp.wait_ge(p_pad, 16)
            node1_in(0, 0)
            node1_in(1, 1)
            with sp.Fori(0, NODE_LOOPS) as i:
                for r in range(2):
                    n = i * 2 + r
                    sp.wait_ge(n_res[1], after(n))
                    node1_in(n + 2, r)
                    node1_out(n, r)
            node1_out(NT - 1, 0)
            sp.wait_ge(n_in[1][1], 32 * (NODE_LOOPS + 1))

        @block.gpsimd
        def _(pool):
            nc.gpsimd.memset(zeros[:, :], 0.0).then_inc(p_fill, 1)
            nc.gpsimd.memset(w1_sb[:, :], 0.0)
            nc.gpsimd.memset(w2_sb[:, :], 0.0)
            nc.gpsimd.memset(w3_sb[:, :], 0.0).then_inc(p_fill, 1)
            nc.gpsimd.memset(ones[:, :], 1.0)
            nc.gpsimd.memset(identity[:, :], 0.0)
            nc.gpsimd.memset(eps_sb[:, :], LN_EPS)
            nc.gpsimd.memset(all_one[:, :], 1.0)
            nc.gpsimd.memset(meta[:, T:T + BLK, :], 0.0).then_inc(p_fill, 1)
            nc.gpsimd.iota(column_no[:, :], pattern=[[1, P]], base=0, channel_multiplier=0,
                           allow_small_or_imprecise_dtypes=True).then_inc(p_fill, 1)
            pool.wait_ge(p_fill, 4)
            nc.gpsimd.affine_select(out=identity[:, :], in_=identity[:, :], compare_op=ALU.not_equal, fill=1.0,
                                    base=0, pattern=[[-1, P]], channel_multiplier=1).then_inc(p_fill, 1)
            nc.gpsimd.affine_select(out=upto[:, :], in_=ones[:, :], compare_op=ALU.is_ge, fill=0.0,
                                    base=0, pattern=[[1, P]], channel_multiplier=-1).then_inc(p_fill, 1)
            for l in range(2):
                pool.sem_inc(e_meta[l], CREDIT)
                pool.sem_inc(e_idx[l], CREDIT)
            pool.sem_inc(n_gm, CREDIT)
            pool.sem_inc(n_gb, CREDIT)

            def meta_block(l, b, h):
                nc.gpsimd.tensor_copy(meta_blk[:, h, :, :], meta[:, bass.ds(b * BLK, BLK), :])
                nc.gpsimd.tensor_copy(y_blk[:, h, :, :], y_sb[:, bass.ds(b * BLK, BLK), :]).then_inc(e_meta[l], 1)

            def gather(l, table, h, k):
                nc.gpsimd.indirect_dma_start(
                    out=rows[:, k, :], out_offset=None, in_=table,
                    in_offset=bass.IndirectOffsetOnAxis(ap=src_blk[:, h, k:k + 1], axis=0),
                ).then_inc(e_row[l][k], 16)

            def edge_stage(l, source, table, width):
                for r in range(AR):
                    pool.dma_start(acc[:, r, :], zeros[:, :]).then_inc(e_out[l][r], 16)
                pool.wait_ge(e_src[l][0], 16)
                for k in range(BLK):
                    gather(l, source, 0, k)
                meta_block(l, 0, 0)
                with pool.Fori(0, LOOPS) as i:
                    for u in range(BODY):
                        t = i * BODY + u
                        r = u % AR
                        h = u // BLK
                        pool.wait_ge(e_side[l], after(t))
                        pool.wait_ge(e_out[l][r], (i * (BODY // AR) + u // AR + 1) * 16)
                        passed(pool)
                        nc.gpsimd.tensor_scalar(row_index[:, r:r + 1], side[:, r, 1:2], SKIP, None,
                                                ALU.add).then_inc(e_idx[l], 1)
                        pool.wait_ge(e_idx[l], after(t))
                        pool.wait_ge(e_acc[l], after(t))
                        passed(pool)
                        nc.gpsimd.indirect_dma_start(
                            out=table, out_offset=bass.IndirectOffsetOnAxis(ap=row_index[:, r:r + 1], axis=0),
                            in_=acc[:, r, 0:width], in_offset=None, bounds_check=N - 1, oob_is_err=False,
                        ).then_inc(e_out[l][r], 16)
                        if u % BLK == 0:
                            meta_block(l, i * 2 + (h + 1), 1 - h)
                            pool.wait_ge(e_src[l][1 - h], (i + (h + 1)) * 16)
                            passed(pool)
                        gather(l, source, 1 - h, u % BLK)

            pool.wait_ge(p_meta, 1)
            pool.wait_ge(p_wts, 16 * 11)
            pool.wait_ge(p_zero, 32)
            edge_stage(0, x, agg_dram, D + 1)

            def affine(n):
                pool.wait_ge(n_norm, after(n))
                nc.gpsimd.tensor_tensor(nhg[:, :], nhn[:, :], gamma_sb[:, :], ALU.mult).then_inc(n_gm, 1)
                pool.wait_ge(n_gm, after(n))
                nc.gpsimd.tensor_tensor(nhb[:, :], nhg[:, :], beta_sb[:, :], ALU.add).then_inc(n_gb, 1)

            with pool.Fori(0, NT) as n:
                affine(n)

            pool.wait_ge(n_stored[0], after(NT - 1))
            edge_stage(1, up_dram[0:NT * P, :], msg_dram, 2 * D)

        @block.scalar
        def _(act):
            for s in (e_side[0], e_side[1], m_picky, m_dot0, n_te[0], n_te[1], n_std[0], n_std[1],
                      n_norm, n_fin[0], n_fin[1], n_x1e, n_up):
                act.sem_inc(s, CREDIT)
            act.wait_ge(p_fill, 1)
            act.dma_start(agg_dram.rearrange("(t p) d -> p t d", p=P),
                          zeros[:, None, 0:D + 1].to_broadcast([P, NT + 1, D + 1])).then_inc(p_zero, 16)
            act.dma_start(msg_dram.rearrange("(t p) d -> p t d", p=P),
                          zeros[:, None, :].to_broadcast([P, NT + 1, 2 * D])).then_inc(p_zero, 16)
            act.dma_start(x1_dram[NT * P:NPAD, :], zeros[:, 0:D]).then_inc(p_pad, 16)
            act.wait_ge(p_w2, 16 * 8)
            nc.scalar.activation(w4_sb[:, 0:3 * MUL], w4_raw[:, 0:3 * MUL], ACT.Copy,
                                 scale=SILU_2MOM / math.sqrt(HID))
            nc.scalar.activation(w4_sb[:, 3 * MUL:D], w4_raw[:, 3 * MUL:D], ACT.Copy,
                                 scale=SILU_2MOM / math.sqrt(HID) / math.sqrt(3.0)).then_inc(p_w4, 1)

            def side_copy(l, t, r):
                act.wait_ge(e_sidep[l], after(t))
                act.wait_ge(e_acc[l], after(t - AR))
                act.wait_ge(e_idx[l], after(t - AR))
                nc.scalar.activation(side[:, r, :], bank[6][:, 0:3], ACT.Copy).then_inc(e_side[l], 1)

            with act.Fori(0, T // AR) as i:
                for r in range(AR):
                    side_copy(0, i * AR + r, r)

            def evac0(n, r):
                act.wait_ge(n_tp[0], n * 2 + (CREDIT + 1))
                nc.scalar.activation(rows[:, r, :], bank[0][:, :], ACT.Copy).then_inc(n_te[0], 1)
                act.wait_ge(n_tp[0], n * 2 + (CREDIT + 2))
                nc.scalar.activation(rows[:, 2 + r, :], bank[1][:, :], ACT.Copy).then_inc(n_te[0], 1)

            def norm0(n, r):
                act.wait_ge(n_var[0], n * 2 + (CREDIT + 1))
                nc.scalar.activation(std[:, :], mv[:, 1:2], ACT.Sqrt, bias=eps_sb[:, :]).then_inc(n_std[0], 1)
                act.wait_ge(n_shift[0], n * 2 + (CREDIT + 1))
                nc.scalar.activation(nhn[:, :], nh[:, :], ACT.Identity, bias=shift[:, :],
                                     scale=rstd[:, :]).then_inc(n_norm, 1)
                act.wait_ge(n_var[0], n * 2 + (CREDIT + 2))
                nc.scalar.activation(std[:, :], mv[:, 1:2], ACT.Sqrt, bias=eps_sb[:, :]).then_inc(n_std[0], 1)
                act.wait_ge(n_shift[0], n * 2 + (CREDIT + 2))
                act.wait_ge(n_stored[0], after(n - 2))
                nc.scalar.activation(nout[:, r, :], nres[:, :], ACT.Identity, bias=shift[:, :],
                                     scale=rstd[:, :]).then_inc(n_fin[0], 1)
                act.wait_ge(n_x1t, after(n))
                nc.scalar.activation(rows[:, 4, :], bank[4][:, :], ACT.Copy).then_inc(n_x1e, 1)
                act.wait_ge(n_upp, after(n))
                nc.scalar.activation(nup[:, r, :], bank[5][:, :], ACT.Copy,
                                     scale=1.0 / math.sqrt(MUL)).then_inc(n_up, 1)

            evac0(0, 0)
            with act.Fori(0, NODE_LOOPS) as i:
                for r in range(2):
                    n = i * 2 + r
                    evac0(n + 1, 1 - r)
                    norm0(n, r)
            norm0(NT - 1, 0)

            def silu(k, o, i_, scale):
                act.wait_ge(m_z, k + 1)
                nc.scalar.activation(o, i_, ACT.Silu, scale=scale).then_inc(m_h, 1)

            inner = SILU_2MOM / math.sqrt(HID)

            def mlp_layer(b, h, k):
                o = (hid1[:, :], hid2[:, :], hid3[:, h, :])[k]
                silu(b * 3 + k, o, bank[7][:, :], 1.0 / math.sqrt(RB) if k == 0 else inner)

            def weigh(t, k, slot, h, c):
                act.wait_ge(e_pick[1], after(t))
                act.wait_ge(e_sum[1], after(t - 2))
                for m in range(4):
                    last = nc.scalar.activation(pick_y[:, k, m, :], pick[:, k, :], ACT.Copy,
                                                scale=y_blk[:, h, c, m:m + 1])
                last.then_inc(m_picky, 1)
                act.wait_ge(e_row[1][slot[0]], slot[1])
                act.wait_ge(m_msg, after(t - 2))
                nc.scalar.activation(dot0[:, k, :], rows[:, slot[0], MUL:2 * MUL], ACT.Copy,
                                     scale=y_blk[:, h, c, 1:2]).then_inc(m_dot0, 1)

            for k in range(3):
                mlp_layer(0, 0, k)
            act.wait_ge(e_meta[1], after(0))
            weigh(0, 0, (0, 16), 0, 0)
            with act.Fori(0, LOOPS) as i:
                for u in range(BODY):
                    t = i * BODY + u
                    v = u + 1
                    h = (v // BLK) % 2
                    if v % BLK == 0:
                        act.wait_ge(e_meta[1], after(i * 2 + v // BLK))
                    weigh(t + 1, v % 2, (v % BLK, (i * 2 + (v // BLK + 1)) * 16), h, v % BLK)
                    side_copy(1, t, u % AR)
                    if u % BLK in (1, 3, 5):
                        b = i * 2 + (u // BLK + 1)
                        mlp_layer(b, (u // BLK + 1) % 2, u % BLK // 2)

            def evac1(n, r):
                act.wait_ge(n_tp[1], n * 2 + (CREDIT + 1))
                nc.scalar.activation(rows[:, 2 * r, :], bank[0][:, :], ACT.Copy).then_inc(n_te[1], 1)

            def norm1(n, r):
                act.wait_ge(n_var[1], after(n))
                nc.scalar.activation(std[:, :], mv[:, 1:2], ACT.Sqrt, bias=eps_sb[:, :]).then_inc(n_std[1], 1)
                act.wait_ge(n_shift[1], after(n))
                act.wait_ge(n_stored[1], after(n - 2))
                nc.scalar.activation(nout[:, r, :], nres[:, :], ACT.Identity, bias=shift[:, :],
                                     scale=rstd[:, :]).then_inc(n_fin[1], 1)

            evac1(0, 0)
            with act.Fori(0, NODE_LOOPS) as i:
                for r in range(2):
                    n = i * 2 + r
                    evac1(n + 1, 1 - r)
                    norm1(n, r)
            norm1(NT - 1, 0)

        @block.vector
        def _(dve):
            for s in (e_pick[0], e_pick[1], e_acc[0], e_acc[1], m_dot, m_msg, n_neigh, n_hread,
                      n_var[0], n_var[1], n_shift[0], n_shift[1], n_res[0], n_res[1], n_te2):
                dve.sem_inc(s, CREDIT)

            dve.wait_ge(p_tab, 48)
            dve.wait_ge(p_fill, 6)
            nc.vector.tensor_tensor(opens[:, :], dst_sb[:, :], before_sb[:, :], ALU.not_equal).then_inc(p_chain, 1)
            nc.vector.tensor_tensor(closes[:, :], dst_sb[:, :], after_sb[:, :], ALU.not_equal).then_inc(p_chain, 1)
            nc.vector.tensor_copy(meta[:, 0:T, 3], all_one[:, :]).then_inc(p_chain, 1)
            dve.wait_ge(p_runs, 1)
            half_t = T // 2
            for k in range(2):
                s = slice(k * half_t, (k + 1) * half_t)
                nc.vector.tensor_copy(runs[:, s], bank[k][:, 0:half_t])
                nc.vector.tensor_copy(run_sum[:, s], bank[2 + k][:, 0:half_t]).then_inc(p_chain, 1)
            dve.wait_ge(p_chain, 5)
            nc.vector.tensor_tensor(runs[:, :], runs[:, :], run_sum[:, :], ALU.subtract).then_inc(p_chain, 1)
            nc.vector.tensor_tensor_scan(all_sum[:, :], all_one[:, :], run_sum[:, :],
                                         0.0, ALU.mult, ALU.add).then_inc(p_chain, 1)
            dve.wait_ge(p_chain, 7)
            nc.vector.tensor_tensor(run_int[:, :], runs[:, :], all_sum[:, :], ALU.add).then_inc(p_chain, 1)
            dve.wait_ge(p_chain, 8)
            nc.vector.tensor_scalar(run_int[:, :], run_int[:, :], P - 1, None, ALU.bitwise_and).then_inc(p_chain, 1)
            dve.wait_ge(p_chain, 9)
            nc.vector.tensor_copy(meta[:, 0:T, 0], run_int[:, :])
            nc.vector.tensor_scalar(all_sum[:, :], opens[:, :], -1.0, 1.0, ALU.mult, ALU.add).then_inc(p_chain, 1)
            nc.vector.scalar_tensor_tensor(meta[:, 0:T, 2], dst_sb[:, :], -SKIP, closes[:, :],
                                           ALU.add, ALU.mult).then_inc(p_chain, 1)
            dve.wait_ge(p_chain, 11)
            nc.vector.tensor_scalar(meta[:, 0:T, 1], all_sum[:, :], identity[:, 0:1], None, ALU.mult).then_inc(p_meta, 1)

            def build_pick(l, t, k, h, c):
                dve.wait_ge(e_sum[l], after(t - 2))
                nc.vector.tensor_scalar(pick[:, k, :], column_no[:, :], meta_blk[:, h, c, 0:1], None,
                                        ALU.is_equal).then_inc(e_pick[l], 1)

            def accumulate(l, t, i, u, banks):
                r = u % AR
                dve.wait_ge(e_side[l], after(t))
                dve.wait_ge(e_sum[l], after(t))
                dve.wait_ge(e_acc[l], after(t - 1))
                dve.wait_ge(e_out[l][r], (i * (BODY // AR) + u // AR + 1) * 16)
                last = (r - 1) % AR
                for c, b in enumerate(banks):
                    s = slice(c * D, (c + 1) * D)
                    ins = nc.vector.scalar_tensor_tensor(acc[:, r, s], acc[:, last, s], side[:, r, 0:1],
                                                         bank[b][:, :], ALU.mult, ALU.add)
                if l == 0:
                    ins = nc.vector.scalar_tensor_tensor(acc[:, r, D:D + 1], acc[:, last, D:D + 1],
                                                         side[:, r, 0:1], side[:, r, 2:3], ALU.mult, ALU.add)
                ins.then_inc(e_acc[l], 1)

            def slots_cleared(l):
                for r in range(AR):
                    dve.wait_ge(e_out[l][r], 16)

            slots_cleared(0)
            dve.wait_ge(e_meta[0], after(0))
            build_pick(0, 0, 0, 0, 0)
            with dve.Fori(0, LOOPS) as i:
                for u in range(BODY):
                    t = i * BODY + u
                    v = u + 1
                    if v % BLK == 0:
                        dve.wait_ge(e_meta[0], after(i * 2 + v // BLK))
                    build_pick(0, t + 1, v % 2, (v // BLK) % 2, v % BLK)
                    accumulate(0, t, i, u, [u % 2])

            def mean_neighbour(n, r, q):
                dve.wait_ge(n_in[0][r], (q + 1) * 32)
                nc.vector.tensor_scalar(cnt[:, :], nagg[:, r, D:D + 1], 1.0, None, ALU.max).then_inc(n_pre, 1)
                dve.wait_ge(n_pre, n * 2 + 1)
                nc.vector.reciprocal(inv[:, :], cnt[:, :]).then_inc(n_pre, 1)
                dve.wait_ge(n_pre, n * 2 + 2)
                nc.vector.tensor_scalar(nneigh[:, r, :], nagg[:, r, 0:D], inv[:, :], None,
                                        ALU.mult).then_inc(n_neigh, 1)

            def norm_factors(l, k):
                nc.vector.reciprocal(rstd[:, :], std[:, :]).then_inc(n_chain[l], 1)
                dve.wait_ge(n_chain[l], k + 1)
                nc.vector.tensor_scalar(shift[:, :], mv[:, 0:1], rstd[:, :], -1.0, ALU.mult,
                                        ALU.mult).then_inc(n_shift[l], 1)

            steps0 = 6

            def update0(n, r):
                dve.wait_ge(n_h[0], after(n))
                nc.vector.tensor_tensor(nh[:, :], bank[2 + r][:, :], bias_sb[:, :], ALU.add).then_inc(n_hread, 1)
                dve.wait_ge(n_hread, after(n))
                nc.vector.bn_stats(stats[:, :], nh[:, :]).then_inc(n_chain[0], 1)
                dve.wait_ge(n_chain[0], n * steps0 + 1)
                passed(dve)
                nc.vector.bn_aggr(mv[:, :], stats[:, :]).then_inc(n_var[0], 1)
                dve.wait_ge(n_std[0], n * 2 + (CREDIT + 1))
                dve.wait_ge(n_fin[0], after(n - 1))
                norm_factors(0, n * steps0 + 1)
                dve.wait_ge(n_gb, after(n))
                nc.vector.tensor_scalar(nlow[:, :], nhb[:, :], 0.0, alpha_sb[:, :], ALU.min,
                                        ALU.mult).then_inc(n_chain[0], 1)
                dve.wait_ge(n_chain[0], n * steps0 + 3)
                nc.vector.scalar_tensor_tensor(nact[:, :], nhb[:, :], 0.0, nlow[:, :], ALU.max,
                                               ALU.add).then_inc(n_chain[0], 1)
                dve.wait_ge(n_chain[0], n * steps0 + 4)
                nc.vector.scalar_tensor_tensor(nres[:, :], nx[:, r, :], 2.0, nact[:, :], ALU.mult,
                                               ALU.add).then_inc(n_res[0], 1)
                dve.wait_ge(n_res[0], after(n))
                nc.vector.bn_stats(stats[:, :], nres[:, :]).then_inc(n_chain[0], 1)
                dve.wait_ge(n_chain[0], n * steps0 + 5)
                passed(dve)
                nc.vector.bn_aggr(mv[:, :], stats[:, :]).then_inc(n_var[0], 1)
                dve.wait_ge(n_std[0], n * 2 + (CREDIT + 2))
                norm_factors(0, n * steps0 + 5)

            dve.wait_ge(p_wts, 16 * 11)
            mean_neighbour(0, 0, 0)
            with dve.Fori(0, NODE_LOOPS) as i:
                for r in range(2):
                    n = i * 2 + r
                    mean_neighbour(n + 1, 1 - r, i + r)
                    update0(n, r)
            update0(NT - 1, 0)

            def messages(t, k, slot, rounds, h, c):
                w = bank[4 + k][:, :].rearrange("p (a v) -> p a v", v=MUL)
                s = rows[:, slot, :].rearrange("p (a v) -> p a v", v=MUL)
                y = y_blk[:, h, c, :]
                dve.wait_ge(m_dot0, after(t))
                dve.wait_ge(e_row[1][slot], rounds)
                nc.vector.scalar_tensor_tensor(dot1[:, :], s[:, 2, :], y[:, 2:3], dot0[:, k, :],
                                               ALU.mult, ALU.add).then_inc(m_dot, 1)
                dve.wait_ge(m_tpw, after(t))
                nc.vector.tensor_tensor(msg[:, k, 0:5:4, :], w[:, 0:2, :],
                                        s[:, 0:1, :].to_broadcast([P, 2, MUL]), ALU.mult)
                dve.wait_ge(m_dot, t * 2 + (CREDIT + 1))
                nc.vector.scalar_tensor_tensor(dot2[:, :], s[:, 3, :], y[:, 3:4], dot1[:, :],
                                               ALU.mult, ALU.add).then_inc(m_dot, 1)
                nc.vector.tensor_tensor(msg[:, k, 1:4, :], w[:, 2:3, :].to_broadcast([P, 3, MUL]),
                                        s[:, 1:4, :], ALU.mult)
                dve.wait_ge(m_dot, t * 2 + (CREDIT + 2))
                nc.vector.tensor_tensor(msg[:, k, 5, :], w[:, 3, :], dot2[:, :], ALU.mult).then_inc(m_msg, 1)

            slots_cleared(1)
            dve.wait_ge(e_meta[1], after(0))
            build_pick(1, 0, 0, 0, 0)
            messages(0, 0, 0, 16, 0, 0)
            with dve.Fori(0, LOOPS) as i:
                for u in range(BODY):
                    t = i * BODY + u
                    v = u + 1
                    h = (v // BLK) % 2
                    if v % BLK == 0:
                        dve.wait_ge(e_meta[1], after(i * 2 + v // BLK))
                    build_pick(1, t + 1, v % 2, h, v % BLK)
                    messages(t + 1, v % 2, v % BLK, (i * 2 + (v // BLK + 1)) * 16, h, v % BLK)
                    accumulate(1, t, i, u, [u % 2, 2 + u % 2])

            def evac1(n, r):
                dve.wait_ge(n_tp[1], n * 2 + (CREDIT + 2))
                nc.vector.tensor_copy(rows[:, 2 * r + 1, :], bank[1][:, :]).then_inc(n_te2, 1)

            def update1(n, r, q):
                scale = 1.0 / math.sqrt(2 * MUL) / AVG_NEIGHBORS
                dve.wait_ge(n_in[1][r], (q + 1) * 32)
                dve.wait_ge(n_h[1], after(n))
                dve.wait_ge(n_fin[1], after(n - 1))
                nc.vector.scalar_tensor_tensor(nres[:, 0:MUL], bank[2 + r][:, 0:MUL], scale, nx[:, r, 0:MUL],
                                               ALU.mult, ALU.add)
                nc.vector.scalar_tensor_tensor(
                    nres[:, MUL:D].rearrange("p (v m) -> p m v", m=3),
                    bank[2 + r][:, MUL:D].rearrange("p (m v) -> p m v", m=3), scale,
                    nx[:, r, MUL:D].rearrange("p (v m) -> p m v", m=3), ALU.mult, ALU.add).then_inc(n_res[1], 1)
                dve.wait_ge(n_res[1], after(n))
                nc.vector.bn_stats(stats[:, :], nres[:, :]).then_inc(n_chain[1], 1)
                dve.wait_ge(n_chain[1], n * 2 + 1)
                passed(dve)
                nc.vector.bn_aggr(mv[:, :], stats[:, :]).then_inc(n_var[1], 1)
                dve.wait_ge(n_std[1], after(n))
                norm_factors(1, n * 2 + 1)

            evac1(0, 0)
            with dve.Fori(0, NODE_LOOPS) as i:
                for r in range(2):
                    n = i * 2 + r
                    evac1(n + 1, 1 - r)
                    update1(n, r, i)
            update1(NT - 1, 0, NODE_LOOPS)

        @block.tensor
        def _(pe):
            for s in (e_sidep[0], e_sidep[1], e_sum[0], e_sum[1], m_tpw, n_tp[0], n_tp[1], n_h[0], n_h[1],
                      n_x1t, n_upp):
                pe.sem_inc(s, CREDIT)

            half_t = T // 2
            pe.wait_ge(p_fill, 6)
            pe.wait_ge(p_chain, 3)
            for k in range(2):
                s = slice(k * half_t, (k + 1) * half_t)
                nc.tensor.matmul(bank[k][:, 0:half_t], upto[:, :], opens[:, s], start=True, stop=True)
                last = nc.tensor.matmul(bank[2 + k][:, 0:half_t], ones[:, :], opens[:, s], start=True, stop=True)
            last.then_inc(p_runs, 1)

            def side_sums(l, t, k, h, c):
                pe.wait_ge(e_pick[l], after(t))
                pe.wait_ge(e_side[l], after(t - 1))
                nc.tensor.matmul(bank[6][:, 0:3], pick[:, k, :], meta_blk[:, h, c, 1:4],
                                 start=True, stop=True).then_inc(e_sidep[l], 1)

            with pe.Fori(0, LOOPS) as i:
                for u in range(BODY):
                    t = i * BODY + u
                    side_sums(0, t, u % 2, u // BLK, u % BLK)
                    pe.wait_ge(e_row[0][u % BLK], (i * 2 + (u // BLK + 1)) * 16)
                    pe.wait_ge(e_acc[0], after(t - 2))
                    nc.tensor.matmul(bank[u % 2][:, :], pick[:, u % 2, :], rows[:, u % BLK, :],
                                     start=True, stop=True).then_inc(e_sum[0], 1)

            def transposes0(n, r, q):
                pe.wait_ge(n_in[0][r], (q + 1) * 32)
                pe.wait_ge(n_te[0], n * 2 + (CREDIT - 1))
                for c in range(4):
                    last = nc.tensor.transpose(bank[0][:, c * P:(c + 1) * P], nx[:, r, c * P:(c + 1) * P], identity[:, :])
                last.then_inc(n_tp[0], 1)
                pe.wait_ge(n_neigh, after(n))
                pe.wait_ge(n_te[0], n * 2 + CREDIT)
                for c in range(4):
                    last = nc.tensor.transpose(bank[1][:, c * P:(c + 1) * P], nneigh[:, r, c * P:(c + 1) * P],
                                               identity[:, :])
                last.then_inc(n_tp[0], 1)

            def products0(n, r):
                pe.wait_ge(n_te[0], n * 2 + (CREDIT + 2))
                pe.wait_ge(n_hread, after(n - 2))
                for c in range(8):
                    w = ws_sb if c < 4 else wn_sb
                    s = slice(c % 4 * P, (c % 4 + 1) * P)
                    last = nc.tensor.matmul(bank[2 + r][:, :], rows[:, 2 * (c // 4) + r, s], w[:, c % 4, :],
                                            start=(c == 0), stop=(c == 7))
                last.then_inc(n_h[0], 1)

            def up0(n, r):
                pe.wait_ge(n_fin[0], after(n))
                pe.wait_ge(n_x1e, after(n - 1))
                for c in range(4):
                    part = nout[:, r, 0:MUL] if c == 0 else nout[:, r, MUL + c - 1:D:3]
                    last = nc.tensor.transpose(bank[4][:, c * P:(c + 1) * P], part, identity[:, :])
                last.then_inc(n_x1t, 1)
                pe.wait_ge(n_x1e, after(n))
                pe.wait_ge(n_up, after(n - 1))
                for c in range(4):
                    last = nc.tensor.matmul(bank[5][:, c * P:(c + 1) * P], rows[:, 4, c * P:(c + 1) * P],
                                            wup_sb[:, min(c, 1), :], start=True, stop=True)
                last.then_inc(n_upp, 1)

            pe.wait_ge(p_wts, 16 * 11)
            transposes0(0, 0, 0)
            products0(0, 0)
            with pe.Fori(0, NODE_LOOPS) as i:
                for r in range(2):
                    n = i * 2 + r
                    transposes0(n + 1, 1 - r, i + r)
                    products0(n + 1, 1 - r)
                    up0(n, r)
            up0(NT - 1, 0)

            def mlp_layer(b, h, rounds, k):
                w, a = ((w1_sb, feats[:, h, :]), (w2_sb, hid1[:, :]), (w3_sb, hid2[:, :]))[k]
                if k == 0:
                    pe.wait_ge(m_feat[h], rounds)
                if not (isinstance(b, int) and b == 0 and k == 0):
                    pe.wait_ge(m_h, b * 3 + k)
                nc.tensor.matmul(bank[7][:, :], w[:, :], a, start=True, stop=True).then_inc(m_z, 1)

            def path_weights(t, k, b, h, c):
                if c == 0:
                    pe.wait_ge(m_h, b * 3 + 3)
                pe.wait_ge(m_msg, after(t - 2))
                lo = c // 4 * HID
                nc.tensor.matmul(bank[4 + k][:, :], hid3[lo:lo + HID, h, c % 4 * P:(c % 4 + 1) * P],
                                 w4_sb[lo:lo + HID, :], start=True, stop=True).then_inc(m_tpw, 1)

            pe.wait_ge(p_w2, 16 * 8)
            pe.wait_ge(p_w4, 1)
            for k in range(3):
                mlp_layer(0, 0, 16, k)
            path_weights(0, 0, 0, 0, 0)
            with pe.Fori(0, LOOPS) as i:
                for u in range(BODY):
                    t = i * BODY + u
                    v = u + 1
                    k = u % 2
                    path_weights(t + 1, v % 2, i * 2 + v // BLK, (v // BLK) % 2, v % BLK)
                    side_sums(1, t, k, u // BLK, u % BLK)
                    pe.wait_ge(m_picky, after(t))
                    pe.wait_ge(m_msg, after(t))
                    pe.wait_ge(e_acc[1], after(t - 2))
                    nc.tensor.matmul(bank[k][:, :], pick_y[:, k, 0, :], msg[:, k, 0:4, :], start=True, stop=True)
                    nc.tensor.matmul(bank[2 + k][:, 0:MUL], pick[:, k, :], msg[:, k, 5, :], start=True, stop=True)
                    for m in range(1, 4):
                        last = nc.tensor.matmul(bank[2 + k][:, m * MUL:(m + 1) * MUL], pick_y[:, k, m, :],
                                                msg[:, k, 4, :], start=True, stop=True)
                    last.then_inc(e_sum[1], 1)
                    if u % BLK in (1, 3, 5):
                        b = i * 2 + (u // BLK + 1)
                        h = (u // BLK + 1) % 2
                        mlp_layer(b, h, (i + (u // BLK + 1)) * 16 if h == 0 else (i + 1) * 16, u % BLK // 2)

            def transposes1(n, r, q):
                pe.wait_ge(n_in[1][r], (q + 1) * 32)
                for half, free in ((0, n_te[1]), (1, n_te2)):
                    pe.wait_ge(free, after(n - 1))
                    for c in range(4):
                        s = slice((half * 4 + c) * P, (half * 4 + c + 1) * P)
                        last = nc.tensor.transpose(bank[half][:, c * P:(c + 1) * P], acc[:, r, s], identity[:, :])
                    last.then_inc(n_tp[1], 1)

            def products1(n, r):
                pe.wait_ge(n_te[1], after(n))
                pe.wait_ge(n_te2, after(n))
                pe.wait_ge(n_res[1], after(n - 2))
                for c in range(4):
                    s = slice(c * P, (c + 1) * P)
                    first, second = (2 * r, 2 * r + 1) if c == 0 else (2 * r + 1, 2 * r)
                    w = 0 if c == 0 else 2
                    nc.tensor.matmul(bank[2 + r][:, s], rows[:, first, s], wout_sb[:, w, :], start=True, stop=False)
                    last = nc.tensor.matmul(bank[2 + r][:, s], rows[:, second, s], wout_sb[:, w + 1, :],
                                            start=False, stop=True)
                last.then_inc(n_h[1], 1)

            transposes1(0, 0, 0)
            products1(0, 0)
            with pe.Fori(0, NODE_LOOPS) as i:
                for r in range(2):
                    n = i * 2 + r
                    transposes1(n + 1, 1 - r, i + r)
                    products1(n + 1, 1 - r)


def kernel(**inputs):
    import numpy as np
    import concourse.bacc as bacc
    from concourse.bass_utils import run_bass_kernel_spmd

    def padded(a, rows, fill=0):
        return np.concatenate([a, np.full((rows - a.shape[0],) + a.shape[1:], fill, a.dtype)])

    def by_tile(a):
        return np.ascontiguousarray(a.reshape((-1, P) + a.shape[1:]).swapaxes(0, 1))

    a = {k: np.asarray(v) for k, v in inputs.items()}
    fill = np.full(1, N, a["dst"].dtype)
    dst = padded(a["dst"], T * P, N)
    feats = padded(a["edge_attr_8"], (NBLK + 2) * BLK * P).reshape(NBLK + 2, 2, BLK * P // 2, RB)
    arrays = {
        "x": padded(a["x"], NPAD),
        "src": by_tile(padded(a["src"], (T + 2 * BLK) * P)),
        "dst": by_tile(dst),
        "dst_before": by_tile(np.concatenate([fill, dst[:-1]])),
        "dst_after": by_tile(np.concatenate([dst[1:], fill])),
        "edge_y": by_tile(padded(a["edge_attr_4"], (T + BLK) * P)),
        "edge_feats": np.ascontiguousarray(feats.transpose(1, 3, 0, 2)).reshape(2 * RB, -1),
        "w_self": a["L0_gnn_W_self"],
        "b_self": a["L0_gnn_b_self"].reshape(1, D),
        "w_neigh": a["L0_gnn_W_neigh"],
        "gamma": a["L0_gnn_gamma"].reshape(1, D),
        "beta": a["L0_gnn_beta"].reshape(1, D),
        "alpha": a["L0_gnn_alpha"].reshape(1, 1),
    }
    for name in ("W_up0", "W_up1", "W_mlp1", "W_mlp2", "W_mlp3", "W_mlp4", "W_out0", "W_out1"):
        arrays[name.lower()] = a["L1_gnn_" + name]

    nc = bacc.Bacc("TRN2", target_bir_lowering=False, num_devices=1)
    args, dram = [], {}
    for name, value in arrays.items():
        dram[f"in_{name}"] = np.ascontiguousarray(value)
        args.append(nc.dram_tensor(f"in_{name}", value.shape, mybir.dt.from_np(value.dtype), kind="ExternalInput").ap())
    args.append(nc.dram_tensor("out_rows", [NT * P, D], fp32, kind="ExternalOutput").ap())
    build(nc, *args)
    r = run_bass_kernel_spmd(nc, [dram], core_ids=[0])
    return r.results[0]["out_rows"][:N]
```

```python
import math
from contextlib import ExitStack

import concourse.bass as bass
from concourse import mybir

N = 6250
E = 100000
D = 512
P = 128
MUL = 128
HID = 64
RB = 8
BLK = 8
BODY = 2 * BLK
T = -(-E // (P * BODY)) * BODY
LOOPS = T // BODY
NBLK = T // BLK
NT = -(-N // P)
NPAD = (NT + 1) * P
NODE_LOOPS = (NT - 1) // 2
GROUP = 4
AHEAD = 3
RING = 4
MLP_STEPS = (1, 3, 5)
AR = 4
SKIP = 8191.0
LN_EPS = 1e-5
SILU_2MOM = 1.679177
AVG_NEIGHBORS = 10.0
CREDIT = 4

fp32 = mybir.dt.float32
i32 = mybir.dt.int32
ALU = mybir.AluOpType
ACT = mybir.ActivationFunctionType


def after(k):
    return k + (CREDIT + 1)


def build(nc, x, src, dst, dst_before, dst_after, edge_y, edge_feats, w_self, b_self, w_neigh,
          gamma, beta, alpha, w_up0, w_up1, w_mlp1, w_mlp2, w_mlp3, w_mlp4, w_out0, w_out1, out):
    ctx = ExitStack()
    with ctx:
        def sb(name, shape, dt=fp32):
            return ctx.enter_context(nc.sbuf_tensor(name, shape, dt))

        def sem(name):
            return ctx.enter_context(nc.semaphore(name))

        def sems(name, n):
            return [sem(f"{name}{k}") for k in range(n)]

        agg_dram = nc.dram_tensor("agg_dram", [NPAD, D + 1], fp32, kind="Internal").ap()
        x1_dram = nc.dram_tensor("x1_dram", [NPAD, D], fp32, kind="Internal").ap()
        up_dram = nc.dram_tensor("up_dram", [NPAD, D], fp32, kind="Internal").ap()
        hid_dram = nc.dram_tensor("hid_dram", [NBLK + 2, P, 512], fp32, kind="Internal").ap()
        msg_dram = nc.dram_tensor("msg_dram", [NPAD, 2 * D], fp32, kind="Internal").ap()

        column_no = sb("column_no", [P, P])
        identity = sb("identity", [P, P])
        upto = sb("upto", [P, P])
        ones = sb("ones", [P, P])
        zeros = sb("zeros", [P, 2 * D])
        dst_sb = sb("dst_sb", [P, T], i32)
        before_sb = sb("before_sb", [P, T], i32)
        after_sb = sb("after_sb", [P, T], i32)
        opens = sb("opens", [P, T])
        closes = sb("closes", [P, T])
        runs = sb("runs", [P, T])
        run_sum = sb("run_sum", [P, T])
        all_one = sb("all_one", [P, T])
        all_sum = sb("all_sum", [P, T])
        run_int = sb("run_int", [P, T], i32)
        group_runs = sb("group_runs", [P, T // GROUP])
        most_runs = sb("most_runs", [P, 1])
        crowded = sb("crowded", [P, 1])
        crowded_int = sb("crowded_int", [P, 1], i32)
        meta = sb("meta", [P, T + BLK, 4])
        y_sb = sb("y_sb", [P, T + BLK, 4])
        meta_blk = sb("meta_blk", [P, 2, BLK, 4])
        y_blk = sb("y_blk", [P, 2, BLK, 4])
        src_blk = sb("src_blk", [P, 2, BLK], i32)
        rows = sb("rows", [P, BLK, D])
        pick = sb("pick", [P, RING, P])
        pick_y = sb("pick_y", [P, RING, 4, P])
        side = sb("side", [P, AR, 3])
        row_index = sb("row_index", [P, AR], i32)
        acc = sb("acc", [P, AR, 2 * D])
        msg = sb("msg", [P, RING, 6, MUL])
        dot0 = sb("dot0", [P, RING, MUL])
        dot1 = sb("dot1", [P, MUL])
        dot2 = sb("dot2", [P, MUL])
        feats = sb("feats", [2 * RB, 2, 512])
        hid1 = sb("hid1", [P, 512])
        hid2 = sb("hid2", [P, 512])
        hid3 = sb("hid3", [P, 2, 512])
        ws_sb = sb("ws_sb", [P, 4, D])
        wn_sb = sb("wn_sb", [P, 4, D])
        wup_sb = sb("wup_sb", [P, 2, MUL])
        w1_sb = sb("w1_sb", [2 * RB, P])
        w2_sb = sb("w2_sb", [P, P])
        w3_sb = sb("w3_sb", [P, P])
        w4_raw = sb("w4_raw", [P, D])
        w4_sb = sb("w4_sb", [P, D])
        wout_sb = sb("wout_sb", [P, 4, MUL])
        bias_sb = sb("bias_sb", [P, D])
        gamma_sb = sb("gamma_sb", [P, D])
        beta_sb = sb("beta_sb", [P, D])
        alpha_sb = sb("alpha_sb", [P, 1])
        eps_sb = sb("eps_sb", [P, 1])
        nx = sb("nx", [P, 2, D])
        nagg = sb("nagg", [P, 2, D + 1])
        nneigh = sb("nneigh", [P, 2, D])
        nh = sb("nh", [P, D])
        nhn = sb("nhn", [P, D])
        nhg = sb("nhg", [P, D])
        nhb = sb("nhb", [P, D])
        nlow = sb("nlow", [P, D])
        nact = sb("nact", [P, D])
        nres = sb("nres", [P, D])
        nout = sb("nout", [P, 2, D])
        nup = sb("nup", [P, 2, D])
        stats = sb("stats", [P, 6])
        mv = sb("mv", [P, 2])
        std = sb("std", [P, 1])
        rstd = sb("rstd", [P, 1])
        shift = sb("shift", [P, 1])
        cnt = sb("cnt", [P, 1])
        inv = sb("inv", [P, 1])

        bank = [ctx.enter_context(nc.psum_tensor(f"bank{k}", [P, 512], fp32)) for k in range(8)]

        gate = sems("gate", 2)
        p_tab = sem("p_tab")
        p_wts = sem("p_wts")
        p_w2 = sem("p_w2")
        p_zero = sem("p_zero")
        p_pad = sem("p_pad")
        p_fill = sem("p_fill")
        p_chain = sem("p_chain")
        p_runs = sem("p_runs")
        p_meta = sem("p_meta")
        p_w4 = sem("p_w4")
        e_src = [sems(f"e{l}_src", 2) for l in range(2)]
        e_meta = [sem(f"e{l}_meta") for l in range(2)]
        e_row = [sems(f"e{l}_row", BLK) for l in range(2)]
        e_pick = [sem(f"e{l}_pick") for l in range(2)]
        e_sum = [sem(f"e{l}_sum") for l in range(2)]
        e_sidep = [sem(f"e{l}_sidep") for l in range(2)]
        e_side = [sem(f"e{l}_side") for l in range(2)]
        e_acc = [sem(f"e{l}_acc") for l in range(2)]
        e_idx = [sem(f"e{l}_idx") for l in range(2)]
        e_out = [sems(f"e{l}_out", AR) for l in range(2)]
        m_feat = sems("m_feat", 2)
        m_z = sem("m_z")
        m_h = sem("m_h")
        m_put = sem("m_put")
        m_kept = sem("m_kept")
        m_hid = sems("m_hid", 2)
        m_tpw = sem("m_tpw")
        m_picky = sem("m_picky")
        m_dot0 = sem("m_dot0")
        m_dot = sem("m_dot")
        m_msg = sem("m_msg")
        n_in = [sems(f"n{l}_in", 2) for l in range(2)]
        n_neigh = sem("n_neigh")
        n_pre = sem("n_pre")
        n_chain = [sem(f"n{l}_chain") for l in range(2)]
        n_tp = [sem(f"n{l}_tp") for l in range(2)]
        n_te = [sem(f"n{l}_te") for l in range(2)]
        n_te2 = sem("n_te2")
        n_h = [sem(f"n{l}_h") for l in range(2)]
        n_hread = sem("n_hread")
        n_var = [sem(f"n{l}_var") for l in range(2)]
        n_std = [sem(f"n{l}_std") for l in range(2)]
        n_shift = [sem(f"n{l}_shift") for l in range(2)]
        n_norm = sem("n_norm")
        n_gm = sem("n_gm")
        n_gb = sem("n_gb")
        n_res = [sem(f"n{l}_res") for l in range(2)]
        n_fin = [sem(f"n{l}_fin") for l in range(2)]
        n_x1t = sem("n_x1t")
        n_x1e = sem("n_x1e")
        n_upp = sem("n_upp")
        n_up = sem("n_up")
        n_st = [sem(f"n{l}_st") for l in range(2)]
        n_stored = [sem(f"n{l}_stored") for l in range(2)]

        block = ctx.enter_context(nc.Block())

        def passed(eng):
            eng.sem_inc(gate[0] if eng is nc.gpsimd else gate[1], 1)

        @block.sync
        def _(sp):
            for s in (*n_stored, m_kept):
                sp.sem_inc(s, CREDIT)
            sp.dma_start(dst_sb[:, :], dst).then_inc(p_tab, 16)
            sp.dma_start(before_sb[:, :], dst_before).then_inc(p_tab, 16)
            sp.dma_start(after_sb[:, :], dst_after).then_inc(p_tab, 16)

            def index_block(l, b, h):
                sp.dma_start(src_blk[:, h, :], src[:, bass.ds(b * BLK, BLK)]).then_inc(e_src[l][h], 16)

            index_block(0, 0, 0)
            index_block(0, 1, 1)
            sp.dma_start(y_sb[:, :, :], edge_y).then_inc(p_wts, 16)
            sp.dma_start(ws_sb[:, :, :], w_self.rearrange("(c p) n -> p c n", p=P)).then_inc(p_wts, 16)
            sp.dma_start(wn_sb[:, :, :], w_neigh.rearrange("(c p) n -> p c n", p=P)).then_inc(p_wts, 16)
            sp.dma_start(wup_sb[:, 0, :], w_up0).then_inc(p_wts, 16)
            sp.dma_start(wup_sb[:, 1, :], w_up1).then_inc(p_wts, 16)
            sp.dma_start(wout_sb[:, 0:2, :], w_out0.rearrange("(c p) n -> p c n", p=P)).then_inc(p_wts, 16)
            sp.dma_start(wout_sb[:, 2:4, :], w_out1.rearrange("(c p) n -> p c n", p=P)).then_inc(p_wts, 16)
            sp.dma_start(bias_sb[:, :], b_self.to_broadcast([P, D])).then_inc(p_wts, 16)
            sp.dma_start(gamma_sb[:, :], gamma.to_broadcast([P, D])).then_inc(p_wts, 16)
            sp.dma_start(beta_sb[:, :], beta.to_broadcast([P, D])).then_inc(p_wts, 16)
            sp.dma_start(alpha_sb[:, :], alpha.to_broadcast([P, 1])).then_inc(p_wts, 16)
            sp.dma_start(w4_raw[0:HID, :], w_mlp4).then_inc(p_w2, 16)
            sp.dma_start(w4_raw[HID:P, :], w_mlp4).then_inc(p_w2, 16)
            sp.wait_ge(p_fill, 2)
            for k in range(2):
                sp.dma_start(w1_sb[k * RB:(k + 1) * RB, k * HID:(k + 1) * HID], w_mlp1).then_inc(p_w2, 16)
                sp.dma_start(w2_sb[k * HID:(k + 1) * HID, k * HID:(k + 1) * HID], w_mlp2).then_inc(p_w2, 16)
                sp.dma_start(w3_sb[k * HID:(k + 1) * HID, k * HID:(k + 1) * HID], w_mlp3).then_inc(p_w2, 16)

            def load_feats(b, h):
                sp.dma_start(feats[:, h, :], edge_feats[:, bass.ds(b * 512, 512)]).then_inc(m_feat[h], 16)

            def load_hid(b, h):
                sp.dma_start(hid3[:, h, :], hid_dram[bass.ds(b, 1), :, :].rearrange("b p e -> p (b e)")
                             ).then_inc(m_hid[h], 16)

            def next_index(l, b, h):
                for r in range(BLK):
                    sp.wait_ge(e_row[l][r], (b + 1) * 16)
                index_block(l, b + 2, h)

            def edges_done(l, group):
                for r in range(BLK):
                    sp.wait_ge(e_row[l][r], 16 * (NBLK + 1))
                for r in range(AR):
                    sp.wait_ge(e_out[l][r], 16 * (T // group // AR + 1))

            load_feats(0, 0)
            load_feats(1, 1)
            with sp.Fori(0, LOOPS) as i:
                for h in range(2):
                    b = i * 2 + h
                    next_index(0, b, h)
                    sp.wait_ge(m_z, after(b * 3))
                    load_feats(b + 2, h)
                    sp.wait_ge(m_h, after(b * 3 + 2))
                    sp.dma_start(hid_dram[bass.ds(b, 1), :, :].rearrange("b p e -> p (b e)"),
                                 hid3[:, h, :]).then_inc(m_put, 16)
                    sp.wait_ge(m_put, (b + 1) * 16)
                    sp.sem_inc(m_kept, 1)
            for h in range(2):
                sp.wait_ge(m_feat[h], 16 * (LOOPS + 1))
            sp.wait_ge(p_meta, 1)
            is_crowded = sp.value_load(crowded_int[0:1, 0:1], min_val=0, max_val=1)
            with sp.If(is_crowded != 0):
                edges_done(0, 1)
            with sp.Else():
                edges_done(0, GROUP)

            def node0_in(n, r):
                sp.dma_start(nx[:, r, :], x[bass.ds(n * P, P), :]).then_inc(n_in[0][r], 16)
                sp.dma_start(nagg[:, r, :], agg_dram[bass.ds(n * P, P), :]).then_inc(n_in[0][r], 16)

            def node0_out(n, r):
                sp.wait_ge(n_fin[0], after(n))
                sp.dma_start(x1_dram[bass.ds(n * P, P), :], nout[:, r, :]).then_inc(n_st[0], 16)
                sp.wait_ge(n_up, after(n))
                sp.dma_start(up_dram[bass.ds(n * P, P), :], nup[:, r, :]).then_inc(n_st[0], 16)
                sp.wait_ge(n_st[0], (n + 1) * 32)
                sp.sem_inc(n_stored[0], 1)

            node0_in(0, 0)
            node0_in(1, 1)
            with sp.Fori(0, NODE_LOOPS) as i:
                for r in range(2):
                    n = i * 2 + r
                    sp.wait_ge(n_res[0], after(n))
                    node0_in(n + 2, r)
                    node0_out(n, r)
            node0_out(NT - 1, 0)
            sp.wait_ge(n_in[0][1], 32 * (NODE_LOOPS + 1))

            index_block(1, 0, 0)
            index_block(1, 1, 1)
            sp.wait_ge(p_pad, 32)
            load_hid(0, 0)
            load_hid(1, 1)
            with sp.Fori(0, LOOPS) as i:
                for h in range(2):
                    b = i * 2 + h
                    next_index(1, b, h)
                    sp.wait_ge(m_tpw, after(b * BLK + (BLK - 1)))
                    load_hid(b + 2, h)
            for h in range(2):
                sp.wait_ge(m_hid[h], 16 * (LOOPS + 1))
            with sp.If(is_crowded != 0):
                edges_done(1, 1)
            with sp.Else():
                edges_done(1, GROUP)

            def node1_in(n, r):
                sp.dma_start(nx[:, r, :], x1_dram[bass.ds(n * P, P), :]).then_inc(n_in[1][r], 16)
                sp.dma_start(acc[:, r, :], msg_dram[bass.ds(n * P, P), :]).then_inc(n_in[1][r], 16)

            def node1_out(n, r):
                sp.wait_ge(n_fin[1], after(n))
                sp.dma_start(out[bass.ds(n * P, P), :], nout[:, r, :]).then_inc(n_st[1], 16)
                sp.wait_ge(n_st[1], (n + 1) * 16)
                sp.sem_inc(n_stored[1], 1)

            node1_in(0, 0)
            node1_in(1, 1)
            with sp.Fori(0, NODE_LOOPS) as i:
                for r in range(2):
                    n = i * 2 + r
                    sp.wait_ge(n_res[1], after(n))
                    node1_in(n + 2, r)
                    node1_out(n, r)
            node1_out(NT - 1, 0)
            sp.wait_ge(n_in[1][1], 32 * (NODE_LOOPS + 1))

        @block.gpsimd
        def _(pool):
            nc.gpsimd.memset(zeros[:, :], 0.0).then_inc(p_fill, 1)
            nc.gpsimd.memset(w1_sb[:, :], 0.0)
            nc.gpsimd.memset(w2_sb[:, :], 0.0)
            nc.gpsimd.memset(w3_sb[:, :], 0.0).then_inc(p_fill, 1)
            nc.gpsimd.memset(ones[:, :], 1.0)
            nc.gpsimd.memset(identity[:, :], 0.0)
            nc.gpsimd.memset(eps_sb[:, :], LN_EPS)
            nc.gpsimd.memset(all_one[:, :], 1.0)
            nc.gpsimd.memset(meta[:, T:T + BLK, :], 0.0).then_inc(p_fill, 1)
            nc.gpsimd.iota(column_no[:, :], pattern=[[1, P]], base=0, channel_multiplier=0,
                           allow_small_or_imprecise_dtypes=True).then_inc(p_fill, 1)
            pool.wait_ge(p_fill, 4)
            nc.gpsimd.affine_select(out=identity[:, :], in_=identity[:, :], compare_op=ALU.not_equal, fill=1.0,
                                    base=0, pattern=[[-1, P]], channel_multiplier=1).then_inc(p_fill, 1)
            nc.gpsimd.affine_select(out=upto[:, :], in_=ones[:, :], compare_op=ALU.is_ge, fill=0.0,
                                    base=0, pattern=[[1, P]], channel_multiplier=-1).then_inc(p_fill, 1)
            for l in range(2):
                pool.sem_inc(e_meta[l], CREDIT)
                pool.sem_inc(e_idx[l], CREDIT)
            pool.sem_inc(n_gm, CREDIT)
            pool.sem_inc(n_gb, CREDIT)

            def meta_block(l, b, h):
                nc.gpsimd.tensor_copy(meta_blk[:, h, :, :], meta[:, bass.ds(b * BLK, BLK), :])
                nc.gpsimd.tensor_copy(y_blk[:, h, :, :], y_sb[:, bass.ds(b * BLK, BLK), :]).then_inc(e_meta[l], 1)

            def gather(l, table, h, k):
                nc.gpsimd.indirect_dma_start(
                    out=rows[:, k, :], out_offset=None, in_=table,
                    in_offset=bass.IndirectOffsetOnAxis(ap=src_blk[:, h, k:k + 1], axis=0),
                ).then_inc(e_row[l][k], 16)

            def edge_stage(l, source, table, width, rows_used, group):
                for r in range(AR):
                    pool.dma_start(acc[:, r, :], zeros[:, :]).then_inc(e_out[l][r], 16)
                pool.wait_ge(e_src[l][0], 16)
                for k in range(BLK):
                    gather(l, source, 0, k)
                meta_block(l, 0, 0)
                with pool.Fori(0, LOOPS) as i:
                    for u in range(BODY):
                        t = i * BODY + u
                        h = u // BLK
                        if u % BLK == 0:
                            pool.wait_ge(e_sum[l], after(t - 1))
                            meta_block(l, i * 2 + (h + 1), 1 - h)
                            pool.wait_ge(e_src[l][1 - h], (i + (h + 1)) * 16)
                        pool.wait_ge(rows_used, after(t))
                        passed(pool)
                        gather(l, source, 1 - h, u % BLK)
                        if u % group == group - 1:
                            g = i * (BODY // group) + u // group
                            r = u // group % AR
                            pool.wait_ge(e_side[l], after(g))
                            pool.wait_ge(e_out[l][r], (i * (BODY // group // AR) + (u // group // AR + 1)) * 16)
                            passed(pool)
                            nc.gpsimd.tensor_scalar(row_index[:, r:r + 1], side[:, r, 1:2], SKIP, None,
                                                    ALU.add).then_inc(e_idx[l], 1)
                            pool.wait_ge(e_idx[l], after(g))
                            pool.wait_ge(e_acc[l], after(g))
                            passed(pool)
                            nc.gpsimd.indirect_dma_start(
                                out=table, out_offset=bass.IndirectOffsetOnAxis(ap=row_index[:, r:r + 1], axis=0),
                                in_=acc[:, r, 0:width], in_offset=None, bounds_check=N - 1, oob_is_err=False,
                            ).then_inc(e_out[l][r], 16)

            pool.wait_ge(p_meta, 1)
            pool.wait_ge(p_wts, 16 * 11)
            pool.wait_ge(p_zero, 32)
            is_crowded = pool.value_load(crowded_int[0:1, 0:1], min_val=0, max_val=1)
            with pool.If(is_crowded != 0):
                edge_stage(0, x, agg_dram, D + 1, e_sum[0], 1)
            with pool.Else():
                edge_stage(0, x, agg_dram, D + 1, e_sum[0], GROUP)

            def affine(n):
                pool.wait_ge(n_norm, after(n))
                nc.gpsimd.tensor_tensor(nhg[:, :], nhn[:, :], gamma_sb[:, :], ALU.mult).then_inc(n_gm, 1)
                pool.wait_ge(n_gm, after(n))
                nc.gpsimd.tensor_tensor(nhb[:, :], nhg[:, :], beta_sb[:, :], ALU.add).then_inc(n_gb, 1)

            with pool.Fori(0, NT) as n:
                affine(n)

            pool.wait_ge(n_stored[0], after(NT - 1))
            with pool.If(is_crowded != 0):
                edge_stage(1, up_dram[0:NT * P, :], msg_dram, 2 * D, m_msg, 1)
            with pool.Else():
                edge_stage(1, up_dram[0:NT * P, :], msg_dram, 2 * D, m_msg, GROUP)

        @block.scalar
        def _(act):
            for s in (m_h, e_side[0], e_side[1], m_picky, m_dot0, n_te[0], n_te[1], n_std[0], n_std[1],
                      n_norm, n_fin[0], n_fin[1], n_x1e, n_up):
                act.sem_inc(s, CREDIT)
            act.wait_ge(p_fill, 1)
            act.dma_start(agg_dram.rearrange("(t p) d -> p t d", p=P),
                          zeros[:, None, 0:D + 1].to_broadcast([P, NT + 1, D + 1])).then_inc(p_zero, 16)
            act.dma_start(msg_dram.rearrange("(t p) d -> p t d", p=P),
                          zeros[:, None, :].to_broadcast([P, NT + 1, 2 * D])).then_inc(p_zero, 16)
            act.dma_start(x1_dram[NT * P:NPAD, :], zeros[:, 0:D]).then_inc(p_pad, 16)
            act.dma_start(hid_dram[NBLK:NBLK + 2, :, :].rearrange("b p e -> p b e"),
                          zeros[:, :].rearrange("p (b e) -> p b e", e=512)).then_inc(p_pad, 16)
            act.wait_ge(p_w2, 16 * 8)
            nc.scalar.activation(w4_sb[:, 0:3 * MUL], w4_raw[:, 0:3 * MUL], ACT.Copy,
                                 scale=SILU_2MOM / math.sqrt(HID))
            nc.scalar.activation(w4_sb[:, 3 * MUL:D], w4_raw[:, 3 * MUL:D], ACT.Copy,
                                 scale=SILU_2MOM / math.sqrt(HID) / math.sqrt(3.0)).then_inc(p_w4, 1)

            def side_copy(l, i, u, group):
                g = i * (BODY // group) + u // group
                r = u // group % AR
                act.wait_ge(e_sidep[l], after(g))
                act.wait_ge(e_acc[l], after(g - AR))
                act.wait_ge(e_idx[l], after(g - AR))
                nc.scalar.activation(side[:, r, :], bank[6][:, 0:3], ACT.Copy).then_inc(e_side[l], 1)

            inner = SILU_2MOM / math.sqrt(HID)

            def mlp_layer(b, h, k):
                act.wait_ge(m_z, after(b * 3 + k))
                if k == 2:
                    act.wait_ge(m_kept, after(b - 2))
                nc.scalar.activation((hid1[:, :], hid2[:, :], hid3[:, h, :])[k], bank[7][:, :], ACT.Silu,
                                     scale=1.0 / math.sqrt(RB) if k == 0 else inner).then_inc(m_h, 1)

            def edge_stage0(group):
                with act.Fori(0, LOOPS) as i:
                    for u in range(BODY):
                        if u % group == group - 1:
                            side_copy(0, i, u, group)
                        if u % BLK in MLP_STEPS:
                            mlp_layer(i * 2 + u // BLK, u // BLK, MLP_STEPS.index(u % BLK))

            act.wait_ge(p_meta, 1)
            is_crowded = act.value_load(crowded_int[0:1, 0:1], min_val=0, max_val=1)
            with act.If(is_crowded != 0):
                edge_stage0(1)
            with act.Else():
                edge_stage0(GROUP)

            def evac0(n, r):
                act.wait_ge(n_tp[0], n * 2 + (CREDIT + 1))
                nc.scalar.activation(rows[:, r, :], bank[0][:, :], ACT.Copy).then_inc(n_te[0], 1)
                act.wait_ge(n_tp[0], n * 2 + (CREDIT + 2))
                nc.scalar.activation(rows[:, 2 + r, :], bank[1][:, :], ACT.Copy).then_inc(n_te[0], 1)

            def norm0(n, r):
                act.wait_ge(n_var[0], n * 2 + (CREDIT + 1))
                nc.scalar.activation(std[:, :], mv[:, 1:2], ACT.Sqrt, bias=eps_sb[:, :]).then_inc(n_std[0], 1)
                act.wait_ge(n_shift[0], n * 2 + (CREDIT + 1))
                nc.scalar.activation(nhn[:, :], nh[:, :], ACT.Identity, bias=shift[:, :],
                                     scale=rstd[:, :]).then_inc(n_norm, 1)
                act.wait_ge(n_var[0], n * 2 + (CREDIT + 2))
                nc.scalar.activation(std[:, :], mv[:, 1:2], ACT.Sqrt, bias=eps_sb[:, :]).then_inc(n_std[0], 1)
                act.wait_ge(n_shift[0], n * 2 + (CREDIT + 2))
                act.wait_ge(n_stored[0], after(n - 2))
                nc.scalar.activation(nout[:, r, :], nres[:, :], ACT.Identity, bias=shift[:, :],
                                     scale=rstd[:, :]).then_inc(n_fin[0], 1)
                act.wait_ge(n_x1t, after(n))
                nc.scalar.activation(rows[:, 4, :], bank[4][:, :], ACT.Copy).then_inc(n_x1e, 1)
                act.wait_ge(n_upp, after(n))
                nc.scalar.activation(nup[:, r, :], bank[5][:, :], ACT.Copy,
                                     scale=1.0 / math.sqrt(MUL)).then_inc(n_up, 1)

            evac0(0, 0)
            with act.Fori(0, NODE_LOOPS) as i:
                for r in range(2):
                    n = i * 2 + r
                    evac0(n + 1, 1 - r)
                    norm0(n, r)
            norm0(NT - 1, 0)

            def weigh(t, k, slot, rounds, h, c):
                act.wait_ge(e_row[1][slot], rounds)
                act.wait_ge(m_msg, after(t - RING))
                nc.scalar.activation(dot0[:, k, :], rows[:, slot, MUL:2 * MUL], ACT.Copy,
                                     scale=y_blk[:, h, c, 1:2]).then_inc(m_dot0, 1)
                act.wait_ge(e_pick[1], after(t))
                act.wait_ge(e_sum[1], after(t - RING))
                for m in range(4):
                    last = nc.scalar.activation(pick_y[:, k, m, :], pick[:, k, :], ACT.Copy,
                                                scale=y_blk[:, h, c, m:m + 1])
                last.then_inc(m_picky, 1)

            def edge_stage1(group):
                act.wait_ge(e_meta[1], after(0))
                weigh(0, 0, 0, 16, 0, 0)
                weigh(1, 1, 1, 16, 0, 1)
                with act.Fori(0, LOOPS) as i:
                    for u in range(BODY):
                        t = i * BODY + u
                        v = u + 2
                        h = (v // BLK) % 2
                        if v % BLK == 0:
                            act.wait_ge(e_meta[1], after(i * 2 + v // BLK))
                        weigh(t + 2, v % RING, v % BLK, (i * 2 + (v // BLK + 1)) * 16, h, v % BLK)
                        if u % group == group - 1:
                            side_copy(1, i, u, group)

            with act.If(is_crowded != 0):
                edge_stage1(1)
            with act.Else():
                edge_stage1(GROUP)

            def evac1(n, r):
                act.wait_ge(n_tp[1], n * 2 + (CREDIT + 1))
                nc.scalar.activation(rows[:, 2 * r, :], bank[0][:, :], ACT.Copy).then_inc(n_te[1], 1)

            def norm1(n, r):
                act.wait_ge(n_var[1], after(n))
                nc.scalar.activation(std[:, :], mv[:, 1:2], ACT.Sqrt, bias=eps_sb[:, :]).then_inc(n_std[1], 1)
                act.wait_ge(n_shift[1], after(n))
                act.wait_ge(n_stored[1], after(n - 2))
                nc.scalar.activation(nout[:, r, :], nres[:, :], ACT.Identity, bias=shift[:, :],
                                     scale=rstd[:, :]).then_inc(n_fin[1], 1)

            evac1(0, 0)
            with act.Fori(0, NODE_LOOPS) as i:
                for r in range(2):
                    n = i * 2 + r
                    evac1(n + 1, 1 - r)
                    norm1(n, r)
            norm1(NT - 1, 0)

        @block.vector
        def _(dve):
            for s in (e_pick[0], e_pick[1], e_acc[0], e_acc[1], m_dot, m_msg, n_neigh, n_hread,
                      n_var[0], n_var[1], n_shift[0], n_shift[1], n_res[0], n_res[1], n_te2):
                dve.sem_inc(s, CREDIT)

            dve.wait_ge(p_tab, 48)
            dve.wait_ge(p_fill, 6)
            nc.vector.tensor_tensor(opens[:, :], dst_sb[:, :], before_sb[:, :], ALU.not_equal).then_inc(p_chain, 1)
            nc.vector.tensor_tensor(closes[:, :], dst_sb[:, :], after_sb[:, :], ALU.not_equal).then_inc(p_chain, 1)
            nc.vector.tensor_copy(meta[:, 0:T, 3], all_one[:, :]).then_inc(p_chain, 1)
            dve.wait_ge(p_runs, 1)
            half_t = T // 2
            for k in range(2):
                s = slice(k * half_t, (k + 1) * half_t)
                nc.vector.tensor_copy(runs[:, s], bank[k][:, 0:half_t])
                nc.vector.tensor_copy(run_sum[:, s], bank[2 + k][:, 0:half_t]).then_inc(p_chain, 1)
            dve.wait_ge(p_chain, 5)
            nc.vector.tensor_tensor(runs[:, :], runs[:, :], run_sum[:, :], ALU.subtract).then_inc(p_chain, 1)
            nc.vector.tensor_tensor_scan(all_sum[:, :], all_one[:, :], run_sum[:, :],
                                         0.0, ALU.mult, ALU.add).then_inc(p_chain, 1)
            dve.wait_ge(p_chain, 7)
            nc.vector.tensor_tensor(run_int[:, :], runs[:, :], all_sum[:, :], ALU.add).then_inc(p_chain, 1)
            dve.wait_ge(p_chain, 8)
            nc.vector.tensor_scalar(run_int[:, :], run_int[:, :], P - 1, None, ALU.bitwise_and).then_inc(p_chain, 1)
            dve.wait_ge(p_chain, 9)
            nc.vector.tensor_copy(meta[:, 0:T, 0], run_int[:, :])
            nc.vector.tensor_scalar(all_sum[:, :], opens[:, :], -1.0, 1.0, ALU.mult, ALU.add).then_inc(p_chain, 1)
            nc.vector.scalar_tensor_tensor(meta[:, 0:T, 2], dst_sb[:, :], -SKIP, closes[:, :],
                                           ALU.add, ALU.mult).then_inc(p_chain, 1)
            nc.vector.tensor_reduce(group_runs[:, :], run_sum[:, :].rearrange("p (g t) -> p g t", t=GROUP),
                                    mybir.AxisListType.X, ALU.add).then_inc(p_chain, 1)
            dve.wait_ge(p_chain, 12)
            nc.vector.tensor_reduce(most_runs[:, :], group_runs[:, :], mybir.AxisListType.X, ALU.max).then_inc(p_chain, 1)
            dve.wait_ge(p_chain, 13)
            nc.vector.tensor_scalar(crowded[:, :], most_runs[:, :], P - 0.5, None, ALU.is_gt).then_inc(p_chain, 1)
            dve.wait_ge(p_chain, 14)
            nc.vector.tensor_copy(crowded_int[:, :], crowded[:, :])
            nc.vector.tensor_scalar(meta[:, 0:T, 1], all_sum[:, :], identity[:, 0:1], None, ALU.mult).then_inc(p_chain, 1)
            dve.wait_ge(p_chain, 15)
            by_group = meta[:, 0:T, 1].rearrange("p (g t) -> p g t", t=GROUP)[:, :, 1:GROUP]
            nc.vector.tensor_scalar(by_group, by_group, crowded[:, :], None, ALU.mult).then_inc(p_meta, 1)

            def build_pick(l, t, k, h, c):
                dve.wait_ge(e_sum[l], after(t - RING))
                nc.vector.tensor_scalar(pick[:, k, :], column_no[:, :], meta_blk[:, h, c, 0:1], None,
                                        ALU.is_equal).then_inc(e_pick[l], 1)

            def next_pick(l, i, u):
                v = u + AHEAD
                if v % BLK == 0:
                    dve.wait_ge(e_meta[l], after(i * 2 + v // BLK))
                build_pick(l, i * BODY + v, v % RING, (v // BLK) % 2, v % BLK)

            def accumulate(l, i, u, group):
                g = i * (BODY // group) + u // group
                r = u // group % AR
                k = u // group % 2
                dve.wait_ge(e_side[l], after(g))
                dve.wait_ge(e_sum[l], after(i * BODY + u))
                dve.wait_ge(e_acc[l], after(g - 1))
                dve.wait_ge(e_out[l][r], (i * (BODY // group // AR) + (u // group // AR + 1)) * 16)
                last = (r - 1) % AR
                for c, b in enumerate((k,) if l == 0 else (k, 2 + k)):
                    s = slice(c * D, (c + 1) * D)
                    ins = nc.vector.scalar_tensor_tensor(acc[:, r, s], acc[:, last, s], side[:, r, 0:1],
                                                         bank[b][:, :], ALU.mult, ALU.add)
                if l == 0:
                    ins = nc.vector.scalar_tensor_tensor(acc[:, r, D:D + 1], acc[:, last, D:D + 1],
                                                         side[:, r, 0:1], side[:, r, 2:3], ALU.mult, ALU.add)
                ins.then_inc(e_acc[l], 1)

            def first_picks(l):
                for r in range(AR):
                    dve.wait_ge(e_out[l][r], 16)
                dve.wait_ge(e_meta[l], after(0))
                for t in range(AHEAD):
                    build_pick(l, t, t, 0, t)

            def edge_stage0(group):
                first_picks(0)
                with dve.Fori(0, LOOPS) as i:
                    for u in range(BODY):
                        next_pick(0, i, u)
                        if u % group == group - 1:
                            accumulate(0, i, u, group)

            dve.wait_ge(p_meta, 1)
            is_crowded = dve.value_load(crowded_int[0:1, 0:1], min_val=0, max_val=1)
            with dve.If(is_crowded != 0):
                edge_stage0(1)
            with dve.Else():
                edge_stage0(GROUP)

            def mean_neighbour(n, r, q):
                dve.wait_ge(n_in[0][r], (q + 1) * 32)
                nc.vector.tensor_scalar(cnt[:, :], nagg[:, r, D:D + 1], 1.0, None, ALU.max).then_inc(n_pre, 1)
                dve.wait_ge(n_pre, n * 2 + 1)
                nc.vector.reciprocal(inv[:, :], cnt[:, :]).then_inc(n_pre, 1)
                dve.wait_ge(n_pre, n * 2 + 2)
                nc.vector.tensor_scalar(nneigh[:, r, :], nagg[:, r, 0:D], inv[:, :], None,
                                        ALU.mult).then_inc(n_neigh, 1)

            def norm_factors(l, k):
                nc.vector.reciprocal(rstd[:, :], std[:, :]).then_inc(n_chain[l], 1)
                dve.wait_ge(n_chain[l], k + 1)
                nc.vector.tensor_scalar(shift[:, :], mv[:, 0:1], rstd[:, :], -1.0, ALU.mult,
                                        ALU.mult).then_inc(n_shift[l], 1)

            steps0 = 6

            def update0(n, r):
                dve.wait_ge(n_h[0], after(n))
                nc.vector.tensor_tensor(nh[:, :], bank[2 + r][:, :], bias_sb[:, :], ALU.add).then_inc(n_hread, 1)
                dve.wait_ge(n_hread, after(n))
                nc.vector.bn_stats(stats[:, :], nh[:, :]).then_inc(n_chain[0], 1)
                dve.wait_ge(n_chain[0], n * steps0 + 1)
                passed(dve)
                nc.vector.bn_aggr(mv[:, :], stats[:, :]).then_inc(n_var[0], 1)
                dve.wait_ge(n_std[0], n * 2 + (CREDIT + 1))
                dve.wait_ge(n_fin[0], after(n - 1))
                norm_factors(0, n * steps0 + 1)
                dve.wait_ge(n_gb, after(n))
                nc.vector.tensor_scalar(nlow[:, :], nhb[:, :], 0.0, alpha_sb[:, :], ALU.min,
                                        ALU.mult).then_inc(n_chain[0], 1)
                dve.wait_ge(n_chain[0], n * steps0 + 3)
                nc.vector.scalar_tensor_tensor(nact[:, :], nhb[:, :], 0.0, nlow[:, :], ALU.max,
                                               ALU.add).then_inc(n_chain[0], 1)
                dve.wait_ge(n_chain[0], n * steps0 + 4)
                nc.vector.scalar_tensor_tensor(nres[:, :], nx[:, r, :], 2.0, nact[:, :], ALU.mult,
                                               ALU.add).then_inc(n_res[0], 1)
                dve.wait_ge(n_res[0], after(n))
                nc.vector.bn_stats(stats[:, :], nres[:, :]).then_inc(n_chain[0], 1)
                dve.wait_ge(n_chain[0], n * steps0 + 5)
                passed(dve)
                nc.vector.bn_aggr(mv[:, :], stats[:, :]).then_inc(n_var[0], 1)
                dve.wait_ge(n_std[0], n * 2 + (CREDIT + 2))
                norm_factors(0, n * steps0 + 5)

            dve.wait_ge(p_wts, 16 * 11)
            mean_neighbour(0, 0, 0)
            with dve.Fori(0, NODE_LOOPS) as i:
                for r in range(2):
                    n = i * 2 + r
                    mean_neighbour(n + 1, 1 - r, i + r)
                    update0(n, r)
            update0(NT - 1, 0)

            def messages(t, k, slot, rounds, h, c):
                w = bank[4 + k % 2][:, :].rearrange("p (a v) -> p a v", v=MUL)
                s = rows[:, slot, :].rearrange("p (a v) -> p a v", v=MUL)
                y = y_blk[:, h, c, :]
                dve.wait_ge(m_dot0, after(t))
                dve.wait_ge(e_row[1][slot], rounds)
                nc.vector.scalar_tensor_tensor(dot1[:, :], s[:, 2, :], y[:, 2:3], dot0[:, k, :],
                                               ALU.mult, ALU.add).then_inc(m_dot, 1)
                dve.wait_ge(m_tpw, after(t))
                dve.wait_ge(e_sum[1], after(t - RING))
                nc.vector.tensor_tensor(msg[:, k, 0:5:4, :], w[:, 0:2, :],
                                        s[:, 0:1, :].to_broadcast([P, 2, MUL]), ALU.mult)
                dve.wait_ge(m_dot, t * 2 + (CREDIT + 1))
                nc.vector.scalar_tensor_tensor(dot2[:, :], s[:, 3, :], y[:, 3:4], dot1[:, :],
                                               ALU.mult, ALU.add).then_inc(m_dot, 1)
                nc.vector.tensor_tensor(msg[:, k, 1:4, :], w[:, 2:3, :].to_broadcast([P, 3, MUL]),
                                        s[:, 1:4, :], ALU.mult)
                dve.wait_ge(m_dot, t * 2 + (CREDIT + 2))
                nc.vector.tensor_tensor(msg[:, k, 5, :], w[:, 3, :], dot2[:, :], ALU.mult).then_inc(m_msg, 1)

            def edge_stage1(group):
                first_picks(1)
                messages(0, 0, 0, 16, 0, 0)
                with dve.Fori(0, LOOPS) as i:
                    for u in range(BODY):
                        v = u + 1
                        messages(i * BODY + v, v % RING, v % BLK, (i * 2 + (v // BLK + 1)) * 16,
                                 (v // BLK) % 2, v % BLK)
                        next_pick(1, i, u)
                        if u % group == group - 1:
                            accumulate(1, i, u, group)

            with dve.If(is_crowded != 0):
                edge_stage1(1)
            with dve.Else():
                edge_stage1(GROUP)

            def evac1(n, r):
                dve.wait_ge(n_tp[1], n * 2 + (CREDIT + 2))
                nc.vector.tensor_copy(rows[:, 2 * r + 1, :], bank[1][:, :]).then_inc(n_te2, 1)

            def update1(n, r, q):
                scale = 1.0 / math.sqrt(2 * MUL) / AVG_NEIGHBORS
                dve.wait_ge(n_in[1][r], (q + 1) * 32)
                dve.wait_ge(n_h[1], after(n))
                dve.wait_ge(n_fin[1], after(n - 1))
                nc.vector.scalar_tensor_tensor(nres[:, 0:MUL], bank[2 + r][:, 0:MUL], scale, nx[:, r, 0:MUL],
                                               ALU.mult, ALU.add)
                nc.vector.scalar_tensor_tensor(
                    nres[:, MUL:D].rearrange("p (v m) -> p m v", m=3),
                    bank[2 + r][:, MUL:D].rearrange("p (m v) -> p m v", m=3), scale,
                    nx[:, r, MUL:D].rearrange("p (v m) -> p m v", m=3), ALU.mult, ALU.add).then_inc(n_res[1], 1)
                dve.wait_ge(n_res[1], after(n))
                nc.vector.bn_stats(stats[:, :], nres[:, :]).then_inc(n_chain[1], 1)
                dve.wait_ge(n_chain[1], n * 2 + 1)
                passed(dve)
                nc.vector.bn_aggr(mv[:, :], stats[:, :]).then_inc(n_var[1], 1)
                dve.wait_ge(n_std[1], after(n))
                norm_factors(1, n * 2 + 1)

            evac1(0, 0)
            with dve.Fori(0, NODE_LOOPS) as i:
                for r in range(2):
                    n = i * 2 + r
                    evac1(n + 1, 1 - r)
                    update1(n, r, i)
            update1(NT - 1, 0, NODE_LOOPS)

        @block.tensor
        def _(pe):
            for s in (m_z, e_sidep[0], e_sidep[1], e_sum[0], e_sum[1], m_tpw, n_tp[0], n_tp[1], n_h[0], n_h[1],
                      n_x1t, n_upp):
                pe.sem_inc(s, CREDIT)

            half_t = T // 2
            pe.wait_ge(p_fill, 6)
            pe.wait_ge(p_chain, 3)
            for k in range(2):
                s = slice(k * half_t, (k + 1) * half_t)
                nc.tensor.matmul(bank[k][:, 0:half_t], upto[:, :], opens[:, s], start=True, stop=True)
                last = nc.tensor.matmul(bank[2 + k][:, 0:half_t], ones[:, :], opens[:, s], start=True, stop=True)
            last.then_inc(p_runs, 1)

            def side_sums(l, i, u, group):
                pe.wait_ge(e_pick[l], after(i * BODY + u))
                if u % group == 0:
                    pe.wait_ge(e_side[l], after(i * (BODY // group) + u // group - 1))
                ins = nc.tensor.matmul(bank[6][:, 0:3], pick[:, u % RING, :], meta_blk[:, u // BLK, u % BLK, 1:4],
                                       start=(u % group == 0), stop=(u % group == group - 1))
                if u % group == group - 1:
                    ins.then_inc(e_sidep[l], 1)

            def bank_free(l, i, u, group):
                if u % group == 0:
                    pe.wait_ge(e_acc[l], after(i * (BODY // group) + u // group - 2))

            def mlp_layer(b, h, rounds, k):
                w, a = ((w1_sb, feats[:, h, :]), (w2_sb, hid1[:, :]), (w3_sb, hid2[:, :]))[k]
                if k == 0:
                    pe.wait_ge(m_feat[h], rounds)
                pe.wait_ge(m_h, after(b * 3 + k - 1))
                nc.tensor.matmul(bank[7][:, :], w[:, :], a, start=True, stop=True).then_inc(m_z, 1)

            def edge_stage0(group):
                with pe.Fori(0, LOOPS) as i:
                    for u in range(BODY):
                        side_sums(0, i, u, group)
                        pe.wait_ge(e_row[0][u % BLK], (i * 2 + (u // BLK + 1)) * 16)
                        bank_free(0, i, u, group)
                        nc.tensor.matmul(bank[u // group % 2][:, :], pick[:, u % RING, :], rows[:, u % BLK, :],
                                         start=(u % group == 0), stop=(u % group == group - 1)).then_inc(e_sum[0], 1)
                        if u % BLK in MLP_STEPS:
                            mlp_layer(i * 2 + u // BLK, u // BLK, (i + 1) * 16, MLP_STEPS.index(u % BLK))

            pe.wait_ge(p_w2, 16 * 8)
            pe.wait_ge(p_meta, 1)
            is_crowded = pe.value_load(crowded_int[0:1, 0:1], min_val=0, max_val=1)
            with pe.If(is_crowded != 0):
                edge_stage0(1)
            with pe.Else():
                edge_stage0(GROUP)

            def transposes0(n, r, q):
                pe.wait_ge(n_in[0][r], (q + 1) * 32)
                pe.wait_ge(n_te[0], n * 2 + (CREDIT - 1))
                for c in range(4):
                    last = nc.tensor.transpose(bank[0][:, c * P:(c + 1) * P], nx[:, r, c * P:(c + 1) * P], identity[:, :])
                last.then_inc(n_tp[0], 1)
                pe.wait_ge(n_neigh, after(n))
                pe.wait_ge(n_te[0], n * 2 + CREDIT)
                for c in range(4):
                    last = nc.tensor.transpose(bank[1][:, c * P:(c + 1) * P], nneigh[:, r, c * P:(c + 1) * P],
                                               identity[:, :])
                last.then_inc(n_tp[0], 1)

            def products0(n, r):
                pe.wait_ge(n_te[0], n * 2 + (CREDIT + 2))
                pe.wait_ge(n_hread, after(n - 2))
                for c in range(8):
                    w = ws_sb if c < 4 else wn_sb
                    s = slice(c % 4 * P, (c % 4 + 1) * P)
                    last = nc.tensor.matmul(bank[2 + r][:, :], rows[:, 2 * (c // 4) + r, s], w[:, c % 4, :],
                                            start=(c == 0), stop=(c == 7))
                last.then_inc(n_h[0], 1)

            def up0(n, r):
                pe.wait_ge(n_fin[0], after(n))
                pe.wait_ge(n_x1e, after(n - 1))
                for c in range(4):
                    part = nout[:, r, 0:MUL] if c == 0 else nout[:, r, MUL + c - 1:D:3]
                    last = nc.tensor.transpose(bank[4][:, c * P:(c + 1) * P], part, identity[:, :])
                last.then_inc(n_x1t, 1)
                pe.wait_ge(n_x1e, after(n))
                pe.wait_ge(n_up, after(n - 1))
                for c in range(4):
                    last = nc.tensor.matmul(bank[5][:, c * P:(c + 1) * P], rows[:, 4, c * P:(c + 1) * P],
                                            wup_sb[:, min(c, 1), :], start=True, stop=True)
                last.then_inc(n_upp, 1)

            pe.wait_ge(p_wts, 16 * 11)
            transposes0(0, 0, 0)
            products0(0, 0)
            with pe.Fori(0, NODE_LOOPS) as i:
                for r in range(2):
                    n = i * 2 + r
                    transposes0(n + 1, 1 - r, i + r)
                    products0(n + 1, 1 - r)
                    up0(n, r)
            up0(NT - 1, 0)

            def path_weights(t, k, rounds, h, c):
                if c == 0:
                    pe.wait_ge(m_hid[h], rounds)
                pe.wait_ge(m_msg, after(t - 2))
                lo = c // 4 * HID
                nc.tensor.matmul(bank[4 + k][:, :], hid3[lo:lo + HID, h, c % 4 * P:(c % 4 + 1) * P],
                                 w4_sb[lo:lo + HID, :], start=True, stop=True).then_inc(m_tpw, 1)

            def edge_stage1(group):
                path_weights(0, 0, 16, 0, 0)
                with pe.Fori(0, LOOPS) as i:
                    for u in range(BODY):
                        t = i * BODY + u
                        v = u + 1
                        path_weights(t + 1, v % 2, (i + (v // BLK // 2 + 1)) * 16, (v // BLK) % 2, v % BLK)
                        side_sums(1, i, u, group)
                        pe.wait_ge(m_picky, after(t))
                        pe.wait_ge(m_msg, after(t))
                        bank_free(1, i, u, group)
                        k = u % RING
                        b = u // group % 2
                        start, stop = u % group == 0, u % group == group - 1
                        nc.tensor.matmul(bank[b][:, :], pick_y[:, k, 0, :], msg[:, k, 0:4, :], start=start, stop=stop)
                        nc.tensor.matmul(bank[2 + b][:, 0:MUL], pick[:, k, :], msg[:, k, 5, :], start=start, stop=False)
                        for m in range(1, 4):
                            last = nc.tensor.matmul(bank[2 + b][:, m * MUL:(m + 1) * MUL], pick_y[:, k, m, :],
                                                    msg[:, k, 4, :], start=False, stop=(stop and m == 3))
                        last.then_inc(e_sum[1], 1)

            pe.wait_ge(p_w4, 1)
            with pe.If(is_crowded != 0):
                edge_stage1(1)
            with pe.Else():
                edge_stage1(GROUP)

            def transposes1(n, r, q):
                pe.wait_ge(n_in[1][r], (q + 1) * 32)
                for half, free in ((0, n_te[1]), (1, n_te2)):
                    pe.wait_ge(free, after(n - 1))
                    for c in range(4):
                        s = slice((half * 4 + c) * P, (half * 4 + c + 1) * P)
                        last = nc.tensor.transpose(bank[half][:, c * P:(c + 1) * P], acc[:, r, s], identity[:, :])
                    last.then_inc(n_tp[1], 1)

            def products1(n, r):
                pe.wait_ge(n_te[1], after(n))
                pe.wait_ge(n_te2, after(n))
                pe.wait_ge(n_res[1], after(n - 2))
                for c in range(4):
                    s = slice(c * P, (c + 1) * P)
                    first, second = (2 * r, 2 * r + 1) if c == 0 else (2 * r + 1, 2 * r)
                    w = 0 if c == 0 else 2
                    nc.tensor.matmul(bank[2 + r][:, s], rows[:, first, s], wout_sb[:, w, :], start=True, stop=False)
                    last = nc.tensor.matmul(bank[2 + r][:, s], rows[:, second, s], wout_sb[:, w + 1, :],
                                            start=False, stop=True)
                last.then_inc(n_h[1], 1)

            transposes1(0, 0, 0)
            products1(0, 0)
            with pe.Fori(0, NODE_LOOPS) as i:
                for r in range(2):
                    n = i * 2 + r
                    transposes1(n + 1, 1 - r, i + r)
                    products1(n + 1, 1 - r)


def kernel(**inputs):
    import numpy as np
    import concourse.bacc as bacc
    from concourse.bass_utils import run_bass_kernel_spmd

    def padded(a, rows, fill=0):
        return np.concatenate([a, np.full((rows - a.shape[0],) + a.shape[1:], fill, a.dtype)])

    def by_tile(a):
        return np.ascontiguousarray(a.reshape((-1, P) + a.shape[1:]).swapaxes(0, 1))

    a = {k: np.asarray(v) for k, v in inputs.items()}
    fill = np.full(1, N, a["dst"].dtype)
    dst = padded(a["dst"], T * P, N)
    feats = padded(a["edge_attr_8"], (NBLK + 2) * BLK * P).reshape(NBLK + 2, 2, BLK * P // 2, RB)
    arrays = {
        "x": padded(a["x"], NPAD),
        "src": by_tile(padded(a["src"], (T + 2 * BLK) * P)),
        "dst": by_tile(dst),
        "dst_before": by_tile(np.concatenate([fill, dst[:-1]])),
        "dst_after": by_tile(np.concatenate([dst[1:], fill])),
        "edge_y": by_tile(padded(a["edge_attr_4"], (T + BLK) * P)),
        "edge_feats": np.ascontiguousarray(feats.transpose(1, 3, 0, 2)).reshape(2 * RB, -1),
        "w_self": a["L0_gnn_W_self"],
        "b_self": a["L0_gnn_b_self"].reshape(1, D),
        "w_neigh": a["L0_gnn_W_neigh"],
        "gamma": a["L0_gnn_gamma"].reshape(1, D),
        "beta": a["L0_gnn_beta"].reshape(1, D),
        "alpha": a["L0_gnn_alpha"].reshape(1, 1),
    }
    for name in ("W_up0", "W_up1", "W_mlp1", "W_mlp2", "W_mlp3", "W_mlp4", "W_out0", "W_out1"):
        arrays[name.lower()] = a["L1_gnn_" + name]

    nc = bacc.Bacc("TRN2", target_bir_lowering=False, num_devices=1)
    args, dram = [], {}
    for name, value in arrays.items():
        dram[f"in_{name}"] = np.ascontiguousarray(value)
        args.append(nc.dram_tensor(f"in_{name}", value.shape, mybir.dt.from_np(value.dtype), kind="ExternalInput").ap())
    args.append(nc.dram_tensor("out_rows", [NT * P, D], fp32, kind="ExternalOutput").ap())
    build(nc, *args)
    r = run_bass_kernel_spmd(nc, [dram], core_ids=[0])
    return r.results[0]["out_rows"][:N]
```

```python
import math
from contextlib import ExitStack

import concourse.bass as bass
from concourse import mybir

N = 6250
E = 100000
D = 512
P = 128
MUL = 128
HID = 64
RB = 8
BLK = 8
BODY = 2 * BLK
T = -(-E // (P * BODY)) * BODY
LOOPS = T // BODY
NBLK = T // BLK
NT = -(-N // P)
NPAD = NT * P
GROUP = 4
AHEAD = 3
RING = 4
MLP_STEPS = (0, 2, 4)
AR = 4
SKIP = 8191.0
LN_EPS = 1e-5
SILU_2MOM = 1.679177
AVG_NEIGHBORS = 10.0
CREDIT = 4

fp32 = mybir.dt.float32
fp32r = mybir.dt.float32r
i32 = mybir.dt.int32
ALU = mybir.AluOpType
ACT = mybir.ActivationFunctionType


def after(k):
    return k + (CREDIT + 1)


def live(i, k):
    return not isinstance(i, int) or 0 <= k < NT


def node_steps(engine, step, before, behind):
    bodies = (NT - before - behind) // 4
    for s in range(behind):
        step(0, s)
    with engine.Fori(0, bodies) as i:
        for j in range(4):
            step(i, behind + j)
    for s in range(behind + 4 * bodies, NT + behind):
        step(0, s)


def build(nc, x, src, dst, dst_before, dst_after, edge_y, edge_feats, w_self, b_self, w_neigh,
          gamma, beta, alpha, w_up0, w_up1, w_mlp1, w_mlp2, w_mlp3, w_mlp4, w_out0, w_out1, out):
    ctx = ExitStack()
    with ctx:
        def sb(name, shape, dt=fp32):
            return ctx.enter_context(nc.sbuf_tensor(name, shape, dt))

        def sem(name):
            return ctx.enter_context(nc.semaphore(name))

        def sems(name, n):
            return [sem(f"{name}{k}") for k in range(n)]

        agg_dram = nc.dram_tensor("agg_dram", [NPAD, D + 1], fp32, kind="Internal").ap()
        x1_dram = nc.dram_tensor("x1_dram", [NPAD, D], fp32, kind="Internal").ap()
        up_dram = nc.dram_tensor("up_dram", [NPAD, D], fp32, kind="Internal").ap()
        hid_dram = nc.dram_tensor("hid_dram", [NBLK + 1, P, BLK * P], fp32r, kind="Internal").ap()
        msg_dram = nc.dram_tensor("msg_dram", [LOOPS * P, 2 * D], fp32, kind="Internal").ap()

        column_no = sb("column_no", [P, P])
        identity = sb("identity", [P, P])
        upto = sb("upto", [P, P])
        ones = sb("ones", [P, P])
        zeros = sb("zeros", [P, 2 * D])
        tables = sb("tables", [P, 10, T])
        dst_sb = tables[:, 0, :].bitcast(i32)
        before_sb = tables[:, 1, :].bitcast(i32)
        after_sb = tables[:, 2, :].bitcast(i32)
        run_int = tables[:, 3, :].bitcast(i32)
        opens = tables[:, 4, :]
        closes = tables[:, 5, :]
        runs = tables[:, 6, :]
        run_sum = tables[:, 7, :]
        all_one = tables[:, 8, :]
        all_sum = tables[:, 9, :]
        group_runs = sb("group_runs", [P, T // GROUP])
        most_runs = sb("most_runs", [P, 1])
        crowded = sb("crowded", [P, 1])
        crowded_int = sb("crowded_int", [P, 1], i32)
        meta = sb("meta", [P, T + BLK, 4])
        y_sb = sb("y_sb", [P, T + BLK, 4])
        meta_blk = sb("meta_blk", [P, 2, BLK, 4])
        y_blk = sb("y_blk", [P, 2, BLK, 4])
        src_blk = sb("src_blk", [P, 2, BLK], i32)
        rows = sb("rows", [P, BLK, D])
        pick = sb("pick", [P, RING, P])
        pick_y = sb("pick_y", [P, RING, 4, P])
        msg = sb("msg", [P, RING, 6, MUL])
        dot0 = sb("dot0", [P, RING, MUL])
        side = sb("side", [P, AR, 3])
        row_index = sb("row_index", [P, AR], i32)
        acc = sb("acc", [P, AR, 2 * D])
        dot1 = sb("dot1", [P, MUL])
        dot2 = sb("dot2", [P, MUL])
        feats = sb("feats", [2 * RB, 2, 512])
        hid1 = sb("hid1", [P, 512])
        hid2 = sb("hid2", [P, 512])
        hid3 = sb("hid3", [P, 512])
        hid_bits = sb("hid_bits", [P, 2, 2, 512], fp32r)
        hid_parts = sb("hid_parts", [P, 2, BLK * P], fp32r)
        ws_sb = sb("ws_sb", [P, 4, D])
        wn_sb = sb("wn_sb", [P, 4, D])
        wup_sb = sb("wup_sb", [P, 2, MUL])
        w1_sb = sb("w1_sb", [2 * RB, P])
        w2_sb = sb("w2_sb", [P, P])
        w3_sb = sb("w3_sb", [P, P])
        w4_raw = sb("w4_raw", [P, D])
        w4_sb = sb("w4_sb", [P, D])
        w4_parts = sb("w4_parts", [P, 2, D], fp32r)
        wout_sb = sb("wout_sb", [P, 4, MUL])
        bias_sb = sb("bias_sb", [P, D])
        gamma_sb = sb("gamma_sb", [P, D])
        beta_sb = sb("beta_sb", [P, D])
        alpha_sb = sb("alpha_sb", [P, 1])
        eps_sb = sb("eps_sb", [P, 1])
        node_bufs = tables[:, :, :].rearrange("p a t -> p (a t)")[:, 0:14 * D].rearrange("p (k d) -> p k d", d=D)
        nneigh, nh, nhn, nhb, nres = (node_bufs[:, 2 * k:2 * k + 2, :] for k in range(5))
        nhg, nlow, nact = (node_bufs[:, k, :] for k in range(10, 13))
        nout = sb("nout", [P, 2, D])
        nup = sb("nup", [P, 2, D])
        stats = sb("stats", [P, 2, 2, 6])
        mv = sb("mv", [P, 2, 2, 2])
        std = sb("std", [P, 2, 2, 1])
        rstd = sb("rstd", [P, 2, 2, 1])
        shift = sb("shift", [P, 2, 2, 1])
        cnt = sb("cnt", [P, 1])
        inv = sb("inv", [P, 1])

        nx = msg[:, :, :, :].rearrange("p r a v -> p r (a v)")[:, :, 0:D]
        nagg = acc[:, :, 0:D + 1]

        bank = [ctx.enter_context(nc.psum_tensor(f"bank{k}", [P, 512], fp32)) for k in range(8)]

        gate = sems("gate", 2)
        p_tab = sem("p_tab")
        p_wts = sem("p_wts")
        p_w2 = sem("p_w2")
        p_zero = sems("p_zero", 2)
        p_pad = sem("p_pad")
        p_y = sem("p_y")
        p_skip = sem("p_skip")
        p_fill = sem("p_fill")
        p_chain = sem("p_chain")
        p_runs = sem("p_runs")
        p_meta = sem("p_meta")
        p_w4 = sem("p_w4")
        e_src = [sems(f"e{l}_src", 2) for l in range(2)]
        e_meta = [sem(f"e{l}_meta") for l in range(2)]
        e_row = [sems(f"e{l}_row", BLK) for l in range(2)]
        e_pick = [sem(f"e{l}_pick") for l in range(2)]
        e_sum = [sem(f"e{l}_sum") for l in range(2)]
        e_sidep = sem("e_sidep")
        e_side = [sem(f"e{l}_side") for l in range(2)]
        e_acc = [sem(f"e{l}_acc") for l in range(2)]
        e_idx = [sem(f"e{l}_idx") for l in range(2)]
        e_out = [sems(f"e{l}_out", AR) for l in range(2)]
        m_feat = sems("m_feat", 2)
        m_z = sem("m_z")
        m_h = sem("m_h")
        m_first = sem("m_first")
        m_split = sem("m_split")
        m_put = sem("m_put")
        m_kept = sem("m_kept")
        m_hid = sems("m_hid", 2)
        m_tpw = sem("m_tpw")
        m_picky = sem("m_picky")
        m_dot0 = sem("m_dot0")
        m_dot = sem("m_dot")
        m_msg = sem("m_msg")
        n_in = [sems(f"n{l}_in", AR) for l in range(2)]
        n_cnt = sem("n_cnt")
        n_inv = sem("n_inv")
        n_neigh = sem("n_neigh")
        n_t0 = sems("n_t0", 2)
        n_t1 = sems("n_t1", 2)
        n_te0 = sems("n_te0", 2)
        n_te1 = sems("n_te1", 2)
        n_h = sems("n_h", 2)
        n_hread = sem("n_hread")
        n_stats = sems("n_stats", 3)
        n_var = sems("n_var", 3)
        n_std = sems("n_std", 3)
        n_rstd = sems("n_rstd", 3)
        n_shift = sems("n_shift", 3)
        n_norm = sems("n_norm", 3)
        n_gm = sem("n_gm")
        n_gb = sem("n_gb")
        n_low = sem("n_low")
        n_act = sem("n_act")
        n_res = sems("n_res", 2)
        n_x1t = sem("n_x1t")
        n_x1e = sem("n_x1e")
        n_upp = sem("n_upp")
        n_up = sem("n_up")
        n_out = [sems(f"n{l}_out", 2) for l in range(2)]
        n_kept = sems("n_kept", 2)
        n_upout = sems("n_upout", 2)
        n_upkept = sem("n_upkept")

        def late(group):
            return 2 if group > 1 else 0

        def scattered(i, q, group):
            extra = 1 if late(group) and q % AR == AR - 1 else 0
            return (i * (BODY // group // AR) + (q // AR + 1 + extra)) * 16

        block = ctx.enter_context(nc.Block())

        def passed(eng):
            eng.sem_inc(gate[0] if eng is nc.gpsimd else gate[1], 1)

        @block.sync
        def _(sp):
            for s in (*n_kept, n_upkept, m_kept):
                sp.sem_inc(s, CREDIT)
            sp.dma_start(dst_sb[:, :], dst).then_inc(p_tab, 16)
            sp.dma_start(before_sb[:, :], dst_before).then_inc(p_tab, 16)
            sp.dma_start(after_sb[:, :], dst_after).then_inc(p_tab, 16)

            def index_block(l, b, h):
                sp.dma_start(src_blk[:, h, :], src[:, bass.ds(b * BLK, BLK)]).then_inc(e_src[l][h], 16)

            index_block(0, 0, 0)
            index_block(0, 1, 1)
            sp.dma_start(y_sb[:, :, :], edge_y).then_inc(p_y, 16)
            sp.dma_start(ws_sb[:, :, :], w_self.rearrange("(c p) n -> p c n", p=P)).then_inc(p_wts, 16)
            sp.dma_start(wn_sb[:, :, :], w_neigh.rearrange("(c p) n -> p c n", p=P)).then_inc(p_wts, 16)
            sp.dma_start(wup_sb[:, 0, :], w_up0).then_inc(p_wts, 16)
            sp.dma_start(wup_sb[:, 1, :], w_up1).then_inc(p_wts, 16)
            sp.dma_start(wout_sb[:, 0:2, :], w_out0.rearrange("(c p) n -> p c n", p=P)).then_inc(p_wts, 16)
            sp.dma_start(wout_sb[:, 2:4, :], w_out1.rearrange("(c p) n -> p c n", p=P)).then_inc(p_wts, 16)
            sp.dma_start(bias_sb[:, :], b_self.to_broadcast([P, D])).then_inc(p_wts, 16)
            sp.dma_start(gamma_sb[:, :], gamma.to_broadcast([P, D])).then_inc(p_wts, 16)
            sp.dma_start(beta_sb[:, :], beta.to_broadcast([P, D])).then_inc(p_wts, 16)
            sp.dma_start(alpha_sb[:, :], alpha.to_broadcast([P, 1])).then_inc(p_wts, 16)
            sp.dma_start(w4_raw[0:HID, :], w_mlp4).then_inc(p_w2, 16)
            sp.dma_start(w4_raw[HID:P, :], w_mlp4).then_inc(p_w2, 16)
            sp.wait_ge(p_fill, 2)
            for k in range(2):
                sp.dma_start(w1_sb[k * RB:(k + 1) * RB, k * HID:(k + 1) * HID], w_mlp1).then_inc(p_w2, 16)
                sp.dma_start(w2_sb[k * HID:(k + 1) * HID, k * HID:(k + 1) * HID], w_mlp2).then_inc(p_w2, 16)
                sp.dma_start(w3_sb[k * HID:(k + 1) * HID, k * HID:(k + 1) * HID], w_mlp3).then_inc(p_w2, 16)

            def load_feats(b, h):
                sp.dma_start(feats[:, h, :], edge_feats[:, bass.ds(b * 512, 512)]).then_inc(m_feat[h], 16)

            def next_index(l, b, h):
                for r in range(BLK):
                    sp.wait_ge(e_row[l][r], (b + 1) * 16)
                index_block(l, b + 2, h)

            def edges_done(l, group):
                for r in range(BLK):
                    sp.wait_ge(e_row[l][r], 16 * (NBLK + 1))
                for r in range(AR):
                    sp.wait_ge(e_out[l][r], scattered(LOOPS, r, group))

            load_feats(0, 0)
            load_feats(1, 1)
            with sp.Fori(0, LOOPS) as i:
                sp.dma_start(msg_dram[bass.ds(i * P, P), :], zeros[:, :]).then_inc(p_zero[1], 16)
                for h in range(2):
                    b = i * 2 + h
                    next_index(0, b, h)
                    sp.wait_ge(m_z, after(b * 3))
                    load_feats(b + 2, h)
                    sp.wait_ge(m_split, after(b))
                    for part in range(2):
                        for half in range(2):
                            sp.dma_start(
                                hid_dram[bass.ds(b, 1), part * HID:(part + 1) * HID, half * 512:(half + 1) * 512]
                                .rearrange("b p e -> p (b e)").bitcast(fp32),
                                hid_bits[half * HID:(half + 1) * HID, h, part, :].bitcast(fp32)).then_inc(m_put, 16)
                    sp.wait_ge(m_put, (b + 1) * 64)
                    sp.sem_inc(m_kept, 1)
            for h in range(2):
                sp.wait_ge(m_feat[h], 16 * (LOOPS + 1))
            sp.wait_ge(p_meta, 1)
            is_crowded = sp.value_load(crowded_int[0:1, 0:1], min_val=0, max_val=1)
            with sp.If(is_crowded != 0):
                edges_done(0, 1)
            with sp.Else():
                edges_done(0, GROUP)

            def rows_of(table, i, k):
                return table[bass.ds((i * 4 + k) * P, P), :]

            def load(l, i, k):
                first, second, sums = (x, agg_dram, nagg) if l == 0 else (x1_dram, msg_dram, acc)
                sp.dma_start(nx[:, k % AR, :], rows_of(first, i, k)).then_inc(n_in[l][k % AR], 16)
                sp.dma_start(sums[:, k % AR, :], rows_of(second, i, k)).then_inc(n_in[l][k % AR], 16)

            def stored(landed, i, k, kept):
                sp.wait_ge(landed[k % 2], (i * 2 + (k // 2 + 1)) * 16)
                sp.sem_inc(kept, 1)

            def step0(i, c):
                s = i * 4 + c
                if live(i, c - 1) and live(i, c + 3):
                    sp.wait_ge(n_res[0], after(s - 1))
                    load(0, i, c + 3)
                if live(i, c - 1):
                    sp.wait_ge(n_norm[1], after(s - 1))
                    sp.dma_start(rows_of(x1_dram, i, c - 1), nout[:, (c - 1) % 2, :]
                                 ).then_inc(n_out[0][(c - 1) % 2], 16)
                if live(i, c - 2):
                    sp.wait_ge(n_up, after(s - 2))
                    sp.dma_start(rows_of(up_dram, i, c - 2), nup[:, c % 2, :]).then_inc(n_upout[c % 2], 16)
                    stored(n_out[0], i, c - 2, n_kept[0])
                if live(i, c - 3):
                    stored(n_upout, i, c - 3, n_upkept)

            for k in range(AR):
                load(0, 0, k)
            node_steps(sp, step0, 3, 3)

            index_block(1, 0, 0)
            index_block(1, 1, 1)
            with sp.Fori(0, LOOPS) as i:
                for h in range(2):
                    next_index(1, i * 2 + h, h)
            for h in range(2):
                sp.wait_ge(m_hid[h], 16 * (LOOPS + 1 - h))
            with sp.If(is_crowded != 0):
                edges_done(1, 1)
            with sp.Else():
                edges_done(1, GROUP)

            def step1(i, c):
                s = i * 4 + c
                if live(i, c) and live(i, c + 4):
                    sp.wait_ge(n_res[1], after(s))
                    load(1, i, c + 4)
                if live(i, c):
                    sp.wait_ge(n_norm[2], after(s))
                    sp.dma_start(rows_of(out, i, c), nout[:, c % 2, :]).then_inc(n_out[1][c % 2], 16)
                if live(i, c - 1):
                    stored(n_out[1], i, c - 1, n_kept[1])

            sp.wait_ge(m_msg, after(T + 1))
            for k in range(4):
                load(1, 0, k)
            node_steps(sp, step1, 4, 1)

        @block.gpsimd
        def _(pool):
            nc.gpsimd.memset(zeros[:, :], 0.0).then_inc(p_fill, 1)
            nc.gpsimd.memset(w1_sb[:, :], 0.0)
            nc.gpsimd.memset(w2_sb[:, :], 0.0)
            nc.gpsimd.memset(w3_sb[:, :], 0.0).then_inc(p_fill, 1)
            nc.gpsimd.memset(ones[:, :], 1.0)
            nc.gpsimd.memset(identity[:, :], 0.0)
            nc.gpsimd.memset(eps_sb[:, :], LN_EPS)
            nc.gpsimd.memset(all_one[:, :], 1.0)
            nc.gpsimd.memset(meta[:, T:T + BLK, :], 0.0).then_inc(p_fill, 1)
            nc.gpsimd.iota(column_no[:, :], pattern=[[1, P]], base=0, channel_multiplier=0,
                           allow_small_or_imprecise_dtypes=True).then_inc(p_fill, 1)
            pool.wait_ge(p_fill, 4)
            nc.gpsimd.affine_select(out=identity[:, :], in_=identity[:, :], compare_op=ALU.not_equal, fill=1.0,
                                    base=0, pattern=[[-1, P]], channel_multiplier=1).then_inc(p_fill, 1)
            nc.gpsimd.affine_select(out=upto[:, :], in_=ones[:, :], compare_op=ALU.is_ge, fill=0.0,
                                    base=0, pattern=[[1, P]], channel_multiplier=-1).then_inc(p_fill, 1)
            for l in range(2):
                pool.sem_inc(e_meta[l], CREDIT)
            pool.sem_inc(n_gm, CREDIT)
            pool.sem_inc(n_gb, CREDIT)

            def meta_block(l, b, h):
                if l == 1:
                    nc.gpsimd.tensor_copy(y_blk[:, h, :, :], y_sb[:, bass.ds(b * BLK, BLK), :])
                nc.gpsimd.tensor_copy(meta_blk[:, h, :, :], meta[:, bass.ds(b * BLK, BLK), :]).then_inc(e_meta[l], 1)

            def gather(l, table, h, k):
                nc.gpsimd.indirect_dma_start(
                    out=rows[:, k, :], out_offset=None, in_=table,
                    in_offset=bass.IndirectOffsetOnAxis(ap=src_blk[:, h, k:k + 1], axis=0),
                ).then_inc(e_row[l][k], 16)

            def load_hid(b, h):
                pool.dma_start(hid_parts[:, h, :], hid_dram[bass.ds(b, 1), :, :].rearrange("b p e -> p (b e)")
                               ).then_inc(m_hid[h], 16)

            def scatter(l, table, width, i, q, group):
                g = i * (BODY // group) + q
                r = q % AR
                pool.wait_ge(e_idx[l], after(g))
                pool.wait_ge(e_acc[l], after(g))
                passed(pool)
                nc.gpsimd.indirect_dma_start(
                    out=table, out_offset=bass.IndirectOffsetOnAxis(ap=row_index[:, r:r + 1], axis=0),
                    in_=acc[:, r, 0:width], in_offset=None, bounds_check=N - 1, oob_is_err=False,
                ).then_inc(e_out[l][r], 16)

            def first_rows(l, source):
                pool.wait_ge(e_src[l][0], 16)
                for k in range(BLK):
                    gather(l, source, 0, k)
                for r in range(AR):
                    pool.dma_start(acc[:, r, :], zeros[:, :]).then_inc(e_out[l][r], 16)
                nc.gpsimd.memset(row_index[:, AR - 1:AR], int(SKIP)).then_inc(p_skip, 1)

            def edge_stage(l, source, table, width, rows_used, group):
                meta_block(l, 0, 0)
                if l == 1:
                    load_hid(0, 0)
                else:
                    pool.wait_ge(p_zero[0], 16)
                pool.wait_ge(p_skip, l + 1)
                with pool.Fori(0, LOOPS) as i:
                    for u in range(BODY):
                        t = i * BODY + u
                        h = u // BLK
                        if u % BLK == 0:
                            pool.wait_ge(e_sum[l], after(t - 1))
                            meta_block(l, i * 2 + (h + 1), 1 - h)
                            pool.wait_ge(e_src[l][1 - h], (i + (h + 1)) * 16)
                            if l == 1:
                                load_hid(i * 2 + (h + 1), 1 - h)
                        pool.wait_ge(rows_used, after(t))
                        passed(pool)
                        gather(l, source, 1 - h, u % BLK)
                        if (u - late(group)) % group == group - 1:
                            scatter(l, table, width, i, (u - late(group)) // group, group)
                if late(group):
                    scatter(l, table, width, LOOPS - 1, BODY // group - 1, group)

            first_rows(0, x)
            pool.wait_ge(p_meta, 1)
            is_crowded = pool.value_load(crowded_int[0:1, 0:1], min_val=0, max_val=1)
            with pool.If(is_crowded != 0):
                edge_stage(0, x, agg_dram, D + 1, e_sum[0], 1)
            with pool.Else():
                edge_stage(0, x, agg_dram, D + 1, e_sum[0], GROUP)

            def step0(i, c):
                if live(i, c):
                    n = i * 4 + c
                    pool.wait_ge(n_norm[0], after(n))
                    nc.gpsimd.tensor_tensor(nhg[:, :], nhn[:, c % 2, :], gamma_sb[:, :], ALU.mult).then_inc(n_gm, 1)
                    pool.wait_ge(n_gm, after(n))
                    pool.wait_ge(n_act, after(n - 2))
                    nc.gpsimd.tensor_tensor(nhb[:, c % 2, :], nhg[:, :], beta_sb[:, :], ALU.add).then_inc(n_gb, 1)

            node_steps(pool, step0, 0, 0)

            pool.wait_ge(p_pad, 16)
            pool.wait_ge(m_kept, after(NBLK - 1))
            pool.wait_ge(n_upkept, after(NT - 1))
            pool.wait_ge(p_zero[1], 16 * LOOPS)
            first_rows(1, up_dram[0:NT * P, :])
            pool.wait_ge(p_y, 16)
            with pool.If(is_crowded != 0):
                edge_stage(1, up_dram[0:NT * P, :], msg_dram, 2 * D, m_msg, 1)
            with pool.Else():
                edge_stage(1, up_dram[0:NT * P, :], msg_dram, 2 * D, m_msg, GROUP)

        @block.scalar
        def _(act):
            for s in (m_h, m_first, m_picky, m_dot0, *n_te0, n_te1[0], *n_std, *n_norm, n_x1e, n_up):
                act.sem_inc(s, CREDIT)
            act.wait_ge(p_fill, 1)
            act.wait_ge(p_tab, 48)
            act.wait_ge(e_row[0][BLK - 1], 16)
            act.dma_start(agg_dram.rearrange("(t p) d -> p t d", p=P),
                          zeros[:, None, 0:D + 1].to_broadcast([P, NT, D + 1])).then_inc(p_zero[0], 16)
            act.dma_start(hid_dram[NBLK, :, :].bitcast(fp32), zeros[:, :]).then_inc(p_pad, 16)
            act.wait_ge(p_w2, 16 * 8)
            nc.scalar.activation(w4_sb[:, 0:3 * MUL], w4_raw[:, 0:3 * MUL], ACT.Copy,
                                 scale=SILU_2MOM / math.sqrt(HID))
            nc.scalar.activation(w4_sb[:, 3 * MUL:D], w4_raw[:, 3 * MUL:D], ACT.Copy,
                                 scale=SILU_2MOM / math.sqrt(HID) / math.sqrt(3.0)).then_inc(p_w4, 1)
            act.wait_ge(p_w4, 1)
            nc.scalar.activation(w4_parts[:, 0, :], w4_sb[:, :], ACT.Copy).then_inc(p_w4, 1)

            inner = SILU_2MOM / math.sqrt(HID)

            def mlp_layer(b, h, k):
                act.wait_ge(m_z, after(b * 3 + k))
                if k == 2:
                    act.wait_ge(m_split, after(b - 1))
                nc.scalar.activation((hid1, hid2, hid3)[k][:, :], bank[7][:, :], ACT.Silu,
                                     scale=1.0 / math.sqrt(RB) if k == 0 else inner).then_inc(m_h, 1)
                if k == 2:
                    act.wait_ge(m_h, after(b * 3 + 2))
                    act.wait_ge(m_kept, after(b - 2))
                    nc.scalar.activation(hid_bits[:, h, 0, :], hid3[:, :], ACT.Copy).then_inc(m_first, 1)

            act.wait_ge(p_fill, 6)
            nc.scalar.activation(cnt[:, :], eps_sb[:, :], ACT.Silu)
            with act.Fori(0, LOOPS) as i:
                for u in range(BODY):
                    if u % BLK - 1 in MLP_STEPS:
                        mlp_layer(i * 2 + u // BLK, u // BLK, MLP_STEPS.index(u % BLK - 1))

            def deviation(norm, kind, i, k):
                n = i * 4 + k
                act.wait_ge(n_var[norm], after(n))
                act.wait_ge(n_rstd[norm], after(n - 2))
                nc.scalar.activation(std[:, kind, k % 2, :], mv[:, kind, k % 2, 1:2], ACT.Sqrt,
                                     bias=eps_sb[:, :]).then_inc(n_std[norm], 1)

            def normed(norm, kind, i, k, o, i_):
                act.wait_ge(n_shift[norm], after(i * 4 + k))
                nc.scalar.activation(o, i_, ACT.Identity, bias=shift[:, kind, k % 2, :],
                                     scale=rstd[:, kind, k % 2, :]).then_inc(n_norm[norm], 1)

            def step0(i, c):
                s = i * 4 + c
                if live(i, c - 2):
                    act.wait_ge(n_x1t, after(s - 2))
                    act.wait_ge(n_upp, after(s - 3))
                    nc.scalar.activation(rows[:, 4, :], bank[4][:, :], ACT.Copy).then_inc(n_x1e, 1)
                if live(i, c + 2):
                    act.wait_ge(n_h[0], after(s))
                    act.wait_ge(n_t0[0], after(s + 2))
                    nc.scalar.activation(rows[:, c % 2, :], bank[0][:, :], ACT.Copy).then_inc(n_te0[0], 1)
                    act.wait_ge(n_t1[0], after(s + 2))
                    nc.scalar.activation(rows[:, 2 + c % 2, :], bank[1][:, :], ACT.Copy).then_inc(n_te1[0], 1)
                if live(i, c):
                    deviation(0, 0, i, c)
                    act.wait_ge(n_gm, after(s - 2))
                    normed(0, 0, i, c, nhn[:, c % 2, :], nh[:, c % 2, :])
                if live(i, c - 2):
                    act.wait_ge(n_upp, after(s - 2))
                    act.wait_ge(n_upkept, after(s - 4))
                    nc.scalar.activation(nup[:, c % 2, :], bank[5][:, :], ACT.Copy,
                                         scale=1.0 / math.sqrt(MUL)).then_inc(n_up, 1)
                if live(i, c - 1):
                    deviation(1, 1, i, c - 1)
                    act.wait_ge(n_x1t, after(s - 3))
                    act.wait_ge(n_kept[0], after(s - 3))
                    normed(1, 1, i, c - 1, nout[:, (c - 1) % 2, :], nres[:, (c - 1) % 2, :])

            for k in range(2):
                act.wait_ge(n_t0[0], after(k))
                nc.scalar.activation(rows[:, k, :], bank[0][:, :], ACT.Copy).then_inc(n_te0[0], 1)
                act.wait_ge(n_t1[0], after(k))
                nc.scalar.activation(rows[:, 2 + k, :], bank[1][:, :], ACT.Copy).then_inc(n_te1[0], 1)
            node_steps(act, step0, 2, 2)

            def weigh(t, k, slot, rounds, h, c):
                act.wait_ge(e_row[1][slot], rounds)
                act.wait_ge(m_msg, after(t - RING))
                nc.scalar.activation(dot0[:, k, :], rows[:, slot, MUL:2 * MUL], ACT.Copy,
                                     scale=y_blk[:, h, c, 1:2]).then_inc(m_dot0, 1)
                act.wait_ge(e_pick[1], after(t))
                act.wait_ge(e_sum[1], after(t - RING))
                for m in range(4):
                    last = nc.scalar.activation(pick_y[:, k, m, :], pick[:, k, :], ACT.Copy,
                                                scale=y_blk[:, h, c, m:m + 1])
                last.then_inc(m_picky, 1)

            act.wait_ge(e_meta[1], after(0))
            for t in range(3):
                weigh(t, t, t, 16, 0, t)
            with act.Fori(0, LOOPS) as i:
                for u in range(BODY):
                    v = u + 3
                    if v % BLK == 0:
                        act.wait_ge(e_meta[1], after(i * 2 + v // BLK))
                    weigh(i * BODY + v, v % RING, v % BLK, (i * 2 + (v // BLK + 1)) * 16, (v // BLK) % 2, v % BLK)

            def first_half(k, n):
                act.wait_ge(n_h[1], after(n - 2))
                act.wait_ge(n_t0[1], after(n))
                nc.scalar.activation(rows[:, 2 * k, :], bank[0][:, :], ACT.Copy).then_inc(n_te0[1], 1)

            def step1(i, c):
                s = i * 4 + c
                if live(i, c + 2):
                    first_half(c % 2, s + 2)
                if live(i, c):
                    deviation(2, 0, i, c)
                    act.wait_ge(n_kept[1], after(s - 2))
                    normed(2, 0, i, c, nout[:, c % 2, :], nres[:, c % 2, :])

            for k in range(2):
                first_half(k, k)
            node_steps(act, step1, 2, 0)

        @block.vector
        def _(dve):
            for s in (*e_pick, *e_side, *e_idx, *e_acc, m_split, m_dot, m_msg, n_cnt, n_inv, n_neigh, n_hread, *n_stats, *n_var, *n_rstd,
                      *n_shift, n_low, n_act, *n_res, n_te1[1]):
                dve.sem_inc(s, CREDIT)

            dve.wait_ge(p_tab, 48)
            dve.wait_ge(p_fill, 6)
            nc.vector.tensor_tensor(opens[:, :], dst_sb[:, :], before_sb[:, :], ALU.not_equal).then_inc(p_chain, 1)
            nc.vector.tensor_tensor(closes[:, :], dst_sb[:, :], after_sb[:, :], ALU.not_equal).then_inc(p_chain, 1)
            nc.vector.tensor_copy(meta[:, 0:T, 3], all_one[:, :]).then_inc(p_chain, 1)
            dve.wait_ge(p_runs, 1)
            half_t = T // 2
            for k in range(2):
                s = slice(k * half_t, (k + 1) * half_t)
                nc.vector.tensor_copy(runs[:, s], bank[k][:, 0:half_t])
                nc.vector.tensor_copy(run_sum[:, s], bank[2 + k][:, 0:half_t]).then_inc(p_chain, 1)
            dve.wait_ge(p_chain, 5)
            nc.vector.tensor_tensor(runs[:, :], runs[:, :], run_sum[:, :], ALU.subtract).then_inc(p_chain, 1)
            nc.vector.tensor_tensor_scan(all_sum[:, :], all_one[:, :], run_sum[:, :],
                                         0.0, ALU.mult, ALU.add).then_inc(p_chain, 1)
            dve.wait_ge(p_chain, 7)
            nc.vector.tensor_tensor(run_int[:, :], runs[:, :], all_sum[:, :], ALU.add).then_inc(p_chain, 1)
            dve.wait_ge(p_chain, 8)
            nc.vector.tensor_scalar(run_int[:, :], run_int[:, :], P - 1, None, ALU.bitwise_and).then_inc(p_chain, 1)
            dve.wait_ge(p_chain, 9)
            nc.vector.tensor_copy(meta[:, 0:T, 0], run_int[:, :])
            nc.vector.tensor_scalar(all_sum[:, :], opens[:, :], -1.0, 1.0, ALU.mult, ALU.add).then_inc(p_chain, 1)
            nc.vector.scalar_tensor_tensor(meta[:, 0:T, 2], dst_sb[:, :], -SKIP, closes[:, :],
                                           ALU.add, ALU.mult).then_inc(p_chain, 1)
            nc.vector.tensor_reduce(group_runs[:, :], run_sum[:, :].rearrange("p (g t) -> p g t", t=GROUP),
                                    mybir.AxisListType.X, ALU.add).then_inc(p_chain, 1)
            dve.wait_ge(p_chain, 12)
            nc.vector.tensor_reduce(most_runs[:, :], group_runs[:, :], mybir.AxisListType.X, ALU.max).then_inc(p_chain, 1)
            dve.wait_ge(p_chain, 13)
            nc.vector.tensor_scalar(crowded[:, :], most_runs[:, :], P - 0.5, None, ALU.is_gt).then_inc(p_chain, 1)
            dve.wait_ge(p_chain, 14)
            nc.vector.tensor_copy(crowded_int[:, :], crowded[:, :])
            nc.vector.tensor_scalar(meta[:, 0:T, 1], all_sum[:, :], identity[:, 0:1], None, ALU.mult).then_inc(p_chain, 1)
            dve.wait_ge(p_chain, 15)
            by_group = meta[:, 0:T, 1].rearrange("p (g t) -> p g t", t=GROUP)[:, :, 1:GROUP]
            nc.vector.tensor_scalar(by_group, by_group, crowded[:, :], None, ALU.mult).then_inc(p_meta, 1)

            def build_pick(l, t, k, h, c):
                dve.wait_ge(e_sum[l], after(t - RING))
                nc.vector.tensor_scalar(pick[:, k, :], column_no[:, :], meta_blk[:, h, c, 0:1], None,
                                        ALU.is_equal).then_inc(e_pick[l], 1)

            def next_pick(l, i, u):
                v = u + AHEAD
                if v % BLK == 0:
                    dve.wait_ge(e_meta[l], after(i * 2 + v // BLK))
                build_pick(l, i * BODY + v, v % RING, (v // BLK) % 2, v % BLK)

            def accumulate(l, i, u, group):
                g = i * (BODY // group) + u // group
                r = u // group % AR
                k = u // group % 2
                sums = meta[:, bass.ds(i * BODY + u, 1), 1:4].rearrange("p t c -> p (t c)")
                if l == 0:
                    dve.wait_ge(e_sidep, after(g))
                    nc.vector.tensor_copy(sums, bank[6][:, 0:3])
                    sums = bank[6][:, 0:3]
                nc.vector.tensor_copy(side[:, r, :], sums).then_inc(e_side[l], 1)
                dve.wait_ge(e_out[l][r], scattered(i, u // group, group))
                nc.vector.tensor_scalar(row_index[:, r:r + 1], sums[:, 1:2], SKIP, None, ALU.add).then_inc(e_idx[l], 1)
                dve.wait_ge(e_side[l], after(g))
                dve.wait_ge(e_sum[l], after(i * BODY + u))
                dve.wait_ge(e_acc[l], after(g - 1))
                last = (r - 1) % AR
                for c, b in enumerate((k,) if l == 0 else (k, 2 + k)):
                    s = slice(c * D, (c + 1) * D)
                    ins = nc.vector.scalar_tensor_tensor(acc[:, r, s], acc[:, last, s], side[:, r, 0:1],
                                                         bank[b][:, :], ALU.mult, ALU.add)
                if l == 0:
                    ins = nc.vector.scalar_tensor_tensor(acc[:, r, D:D + 1], acc[:, last, D:D + 1],
                                                         side[:, r, 0:1], side[:, r, 2:3], ALU.mult, ALU.add)
                ins.then_inc(e_acc[l], 1)

            def first_picks(l):
                for r in range(AR):
                    dve.wait_ge(e_out[l][r], 16)
                dve.wait_ge(e_meta[l], after(0))
                for t in range(AHEAD):
                    build_pick(l, t, t, 0, t)

            def split_hidden(b, h):
                dve.wait_ge(m_first, after(b))
                dve.wait_ge(m_kept, after(b - 2))
                nc.vector.tensor_tensor(hid_bits[:, h, 1, :], hid3[:, :], hid_bits[:, h, 0, :].bitcast(fp32),
                                        ALU.subtract).then_inc(m_split, 1)

            def edge_stage0(group):
                first_picks(0)
                with dve.Fori(0, LOOPS) as i:
                    for u in range(BODY):
                        next_pick(0, i, u)
                        if u % group == group - 1:
                            accumulate(0, i, u, group)
                        if u % BLK == BLK - 1:
                            split_hidden(i * 2 + u // BLK, u // BLK)

            dve.wait_ge(p_w4, 2)
            nc.vector.tensor_tensor(w4_parts[:, 1, :], w4_sb[:, :], w4_parts[:, 0, :].bitcast(fp32),
                                    ALU.subtract).then_inc(p_w4, 1)
            dve.wait_ge(p_meta, 1)
            is_crowded = dve.value_load(crowded_int[0:1, 0:1], min_val=0, max_val=1)
            with dve.If(is_crowded != 0):
                edge_stage0(1)
            with dve.Else():
                edge_stage0(GROUP)

            def mean_neighbour(i, k):
                n = i * 4 + k
                dve.wait_ge(n_in[0][k % AR], (i + (k // AR + 1)) * 32)
                nc.vector.tensor_scalar(cnt[:, :], nagg[:, k % AR, D:D + 1], 1.0, None, ALU.max).then_inc(n_cnt, 1)
                dve.wait_ge(n_cnt, after(n))
                nc.vector.reciprocal(inv[:, :], cnt[:, :]).then_inc(n_inv, 1)
                dve.wait_ge(n_inv, after(n))
                dve.wait_ge(n_t1[0], after(n - 2))
                nc.vector.tensor_scalar(nneigh[:, k % 2, :], nagg[:, k % AR, 0:D], inv[:, :], None,
                                        ALU.mult).then_inc(n_neigh, 1)

            def moments(norm, kind, i, k, rows_):
                n = i * 4 + k
                nc.vector.bn_stats(stats[:, kind, k % 2, :], rows_).then_inc(n_stats[norm], 1)
                dve.wait_ge(n_stats[norm], after(n))
                passed(dve)
                nc.vector.bn_aggr(mv[:, kind, k % 2, :], stats[:, kind, k % 2, :]).then_inc(n_var[norm], 1)

            def norm_factors(norm, kind, i, k):
                n = i * 4 + k
                dve.wait_ge(n_std[norm], after(n))
                dve.wait_ge(n_norm[norm], after(n - 2))
                nc.vector.reciprocal(rstd[:, kind, k % 2, :], std[:, kind, k % 2, :]).then_inc(n_rstd[norm], 1)
                dve.wait_ge(n_rstd[norm], after(n))
                nc.vector.tensor_scalar(shift[:, kind, k % 2, :], mv[:, kind, k % 2, 0:1], rstd[:, kind, k % 2, :], -1.0,
                                        ALU.mult, ALU.mult).then_inc(n_shift[norm], 1)

            def step0(i, c):
                s = i * 4 + c
                if live(i, c + 2):
                    mean_neighbour(i, c + 2)
                if live(i, c):
                    dve.wait_ge(n_h[0], after(s))
                    dve.wait_ge(n_norm[0], after(s - 2))
                    nc.vector.tensor_tensor(nh[:, c % 2, :], bank[2 + c % 2][:, :], bias_sb[:, :],
                                            ALU.add).then_inc(n_hread, 1)
                    dve.wait_ge(n_hread, after(s))
                    moments(0, 0, i, c, nh[:, c % 2, :])
                if live(i, c - 1):
                    k = (c - 1) % 2
                    dve.wait_ge(n_gb, after(s - 1))
                    nc.vector.tensor_scalar(nlow[:, :], nhb[:, k, :], 0.0, alpha_sb[:, :], ALU.min,
                                            ALU.mult).then_inc(n_low, 1)
                if live(i, c):
                    norm_factors(0, 0, i, c)
                if live(i, c - 1):
                    dve.wait_ge(n_low, after(s - 1))
                    nc.vector.scalar_tensor_tensor(nact[:, :], nhb[:, k, :], 0.0, nlow[:, :], ALU.max,
                                                   ALU.add).then_inc(n_act, 1)
                    dve.wait_ge(n_act, after(s - 1))
                    dve.wait_ge(n_norm[1], after(s - 3))
                    nc.vector.scalar_tensor_tensor(nres[:, k, :], nx[:, (c - 1) % AR, :], 2.0, nact[:, :], ALU.mult,
                                                   ALU.add).then_inc(n_res[0], 1)
                    dve.wait_ge(n_res[0], after(s - 1))
                    moments(1, 1, i, c - 1, nres[:, k, :])
                    norm_factors(1, 1, i, c - 1)

            dve.wait_ge(p_wts, 16 * 10)
            for k in range(2):
                mean_neighbour(0, k)
            node_steps(dve, step0, 2, 1)

            def messages(t, k, slot, rounds, h, c):
                w = bank[4 + k % 2][:, :].rearrange("p (a v) -> p a v", v=MUL)
                s = rows[:, slot, :].rearrange("p (a v) -> p a v", v=MUL)
                y = y_blk[:, h, c, :]
                dve.wait_ge(m_dot0, after(t))
                dve.wait_ge(e_row[1][slot], rounds)
                nc.vector.scalar_tensor_tensor(dot1[:, :], s[:, 2, :], y[:, 2:3], dot0[:, k, :],
                                               ALU.mult, ALU.add).then_inc(m_dot, 1)
                dve.wait_ge(m_tpw, after(t))
                dve.wait_ge(e_sum[1], after(t - RING))
                nc.vector.tensor_tensor(msg[:, k, 0:5:4, :], w[:, 0:2, :],
                                        s[:, 0:1, :].to_broadcast([P, 2, MUL]), ALU.mult)
                dve.wait_ge(m_dot, t * 2 + (CREDIT + 1))
                nc.vector.scalar_tensor_tensor(dot2[:, :], s[:, 3, :], y[:, 3:4], dot1[:, :],
                                               ALU.mult, ALU.add).then_inc(m_dot, 1)
                nc.vector.tensor_tensor(msg[:, k, 1:4, :], w[:, 2:3, :].to_broadcast([P, 3, MUL]),
                                        s[:, 1:4, :], ALU.mult)
                dve.wait_ge(m_dot, t * 2 + (CREDIT + 2))
                nc.vector.tensor_tensor(msg[:, k, 5, :], w[:, 3, :], dot2[:, :], ALU.mult).then_inc(m_msg, 1)

            def edge_stage1(group):
                first_picks(1)
                for t in range(2):
                    messages(t, t, t, 16, 0, t)
                with dve.Fori(0, LOOPS) as i:
                    for u in range(BODY):
                        v = u + 2
                        messages(i * BODY + v, v % RING, v % BLK, (i * 2 + (v // BLK + 1)) * 16,
                                 (v // BLK) % 2, v % BLK)
                        next_pick(1, i, u)
                        if u % group == group - 1:
                            accumulate(1, i, u, group)

            with dve.If(is_crowded != 0):
                edge_stage1(1)
            with dve.Else():
                edge_stage1(GROUP)

            def second_half(k, n):
                dve.wait_ge(n_h[1], after(n - 2))
                dve.wait_ge(n_t1[1], after(n))
                nc.vector.tensor_copy(rows[:, 2 * k + 1, :], bank[1][:, :]).then_inc(n_te1[1], 1)

            def step1(i, c):
                s = i * 4 + c
                if live(i, c + 2):
                    second_half(c % 2, s + 2)
                if live(i, c):
                    scale = 1.0 / math.sqrt(2 * MUL) / AVG_NEIGHBORS
                    k, r = c % 2, c % AR
                    dve.wait_ge(n_in[1][r], (i + (c // AR + 1)) * 32)
                    dve.wait_ge(n_h[1], after(s))
                    dve.wait_ge(n_norm[2], after(s - 2))
                    nc.vector.scalar_tensor_tensor(nres[:, k, 0:MUL], bank[2 + k][:, 0:MUL], scale, nx[:, r, 0:MUL],
                                                   ALU.mult, ALU.add)
                    nc.vector.scalar_tensor_tensor(
                        nres[:, k, MUL:D].rearrange("p (v m) -> p m v", m=3),
                        bank[2 + k][:, MUL:D].rearrange("p (m v) -> p m v", m=3), scale,
                        nx[:, r, MUL:D].rearrange("p (v m) -> p m v", m=3), ALU.mult, ALU.add).then_inc(n_res[1], 1)
                    dve.wait_ge(n_res[1], after(s))
                    moments(2, 0, i, c, nres[:, k, :])
                    norm_factors(2, 0, i, c)

            for k in range(2):
                second_half(k, k)
            node_steps(dve, step1, 2, 0)

        @block.tensor
        def _(pe):
            for s in (m_z, e_sidep, *e_sum, m_tpw, *n_t0, *n_t1, *n_h, n_x1t, n_upp):
                pe.sem_inc(s, CREDIT)

            half_t = T // 2
            pe.wait_ge(p_fill, 6)
            pe.wait_ge(p_chain, 3)
            for k in range(2):
                s = slice(k * half_t, (k + 1) * half_t)
                nc.tensor.matmul(bank[k][:, 0:half_t], upto[:, :], opens[:, s], start=True, stop=True)
                last = nc.tensor.matmul(bank[2 + k][:, 0:half_t], ones[:, :], opens[:, s], start=True, stop=True)
            last.then_inc(p_runs, 1)

            def side_sums(i, u, group):
                pe.wait_ge(e_pick[0], after(i * BODY + u))
                if u % group == 0:
                    pe.wait_ge(e_idx[0], after(i * (BODY // group) + u // group - 1))
                ins = nc.tensor.matmul(bank[6][:, 0:3], pick[:, u % RING, :], meta_blk[:, u // BLK, u % BLK, 1:4],
                                       start=(u % group == 0), stop=(u % group == group - 1))
                if u % group == group - 1:
                    ins.then_inc(e_sidep, 1)

            def bank_free(l, i, u, group):
                if u % group == 0:
                    pe.wait_ge(e_acc[l], after(i * (BODY // group) + u // group - 2))

            def mlp_layer(b, h, rounds, k):
                if k == 0:
                    pe.wait_ge(m_feat[h], rounds)
                pe.wait_ge(m_h, after(b * 3 + k - 1))
                w, a = ((w1_sb, feats[:, h, :]), (w2_sb, hid1[:, :]), (w3_sb, hid2[:, :]))[k]
                nc.tensor.matmul(bank[7][:, :], w[:, :], a, start=True, stop=True).then_inc(m_z, 1)

            def edge_stage0(group):
                with pe.Fori(0, LOOPS) as i:
                    for u in range(BODY):
                        side_sums(i, u, group)
                        pe.wait_ge(e_row[0][u % BLK], (i * 2 + (u // BLK + 1)) * 16)
                        bank_free(0, i, u, group)
                        nc.tensor.matmul(bank[u // group % 2][:, :], pick[:, u % RING, :], rows[:, u % BLK, :],
                                         start=(u % group == 0), stop=(u % group == group - 1)).then_inc(e_sum[0], 1)
                        if u % BLK in MLP_STEPS:
                            mlp_layer(i * 2 + u // BLK, u // BLK, (i + 1) * 16, MLP_STEPS.index(u % BLK))

            pe.wait_ge(p_w2, 16 * 8)
            pe.wait_ge(p_meta, 1)
            is_crowded = pe.value_load(crowded_int[0:1, 0:1], min_val=0, max_val=1)
            with pe.If(is_crowded != 0):
                edge_stage0(1)
            with pe.Else():
                edge_stage0(GROUP)

            def transposed(to, parts, n, free, done):
                pe.wait_ge(free, after(n - 1))
                for c, part in enumerate(parts):
                    last = nc.tensor.transpose(to[:, c * P:(c + 1) * P], part, identity[:, :])
                last.then_inc(done, 1)

            def quarters(a):
                return [a[:, c * P:(c + 1) * P] for c in range(4)]

            def transposes0(i, k):
                n = i * 4 + k
                pe.wait_ge(n_in[0][k % AR], (i + (k // AR + 1)) * 32)
                transposed(bank[0], quarters(nx[:, k % AR, :]), n, n_te0[0], n_t0[0])
                pe.wait_ge(n_neigh, after(n))
                transposed(bank[1], quarters(nneigh[:, k % 2, :]), n, n_te1[0], n_t1[0])

            def products0(n, k):
                pe.wait_ge(n_te0[0], after(n))
                pe.wait_ge(n_te1[0], after(n))
                pe.wait_ge(n_hread, after(n - 2))
                for c in range(8):
                    w = ws_sb if c < 4 else wn_sb
                    s = slice(c % 4 * P, (c % 4 + 1) * P)
                    last = nc.tensor.matmul(bank[2 + k][:, :], rows[:, 2 * (c // 4) + k, s], w[:, c % 4, :],
                                            start=(c == 0), stop=(c == 7))
                last.then_inc(n_h[0], 1)

            def step0(i, c):
                s = i * 4 + c
                if live(i, c - 2):
                    x1 = nout[:, c % 2, :]
                    pe.wait_ge(n_norm[1], after(s - 2))
                    transposed(bank[4], [x1[:, 0:MUL]] + [x1[:, MUL + m:D:3] for m in range(3)],
                               s - 2, n_x1e, n_x1t)
                if live(i, c + 2):
                    transposes0(i, c + 2)
                if live(i, c - 2):
                    pe.wait_ge(n_x1e, after(s - 2))
                    pe.wait_ge(n_up, after(s - 3))
                    for m in range(4):
                        last = nc.tensor.matmul(bank[5][:, m * P:(m + 1) * P], rows[:, 4, m * P:(m + 1) * P],
                                                wup_sb[:, min(m, 1), :], start=True, stop=True)
                    last.then_inc(n_upp, 1)
                if live(i, c + 1):
                    products0(s + 1, (c + 1) % 2)

            pe.wait_ge(p_wts, 16 * 10)
            for k in range(2):
                transposes0(0, k)
            products0(0, 0)
            node_steps(pe, step0, 2, 2)

            def path_weights(t, k, rounds, h, c):
                if c == 0:
                    pe.wait_ge(m_hid[h], rounds)
                pe.wait_ge(m_msg, after(t - 2))
                for part in range(2):
                    last = nc.tensor.matmul(bank[4 + k][:, :], hid_parts[:, h, c * P:(c + 1) * P], w4_parts[:, part, :],
                                            start=(part == 0), stop=(part == 1))
                last.then_inc(m_tpw, 1)

            def edge_stage1(group):
                for t in range(2):
                    path_weights(t, t, 16, 0, t)
                with pe.Fori(0, LOOPS) as i:
                    for u in range(BODY):
                        t = i * BODY + u
                        v = u + 2
                        path_weights(t + 2, v % 2, (i + (v // BLK // 2 + 1)) * 16, (v // BLK) % 2, v % BLK)
                        pe.wait_ge(m_picky, after(t))
                        pe.wait_ge(m_msg, after(t))
                        bank_free(1, i, u, group)
                        k = u % RING
                        b = u // group % 2
                        start, stop = u % group == 0, u % group == group - 1
                        nc.tensor.matmul(bank[b][:, :], pick_y[:, k, 0, :], msg[:, k, 0:4, :], start=start, stop=stop)
                        nc.tensor.matmul(bank[2 + b][:, 0:MUL], pick[:, k, :], msg[:, k, 5, :], start=start, stop=False)
                        for m in range(1, 4):
                            last = nc.tensor.matmul(bank[2 + b][:, m * MUL:(m + 1) * MUL], pick_y[:, k, m, :],
                                                    msg[:, k, 4, :], start=False, stop=(stop and m == 3))
                        last.then_inc(e_sum[1], 1)

            pe.wait_ge(p_w4, 3)
            with pe.If(is_crowded != 0):
                edge_stage1(1)
            with pe.Else():
                edge_stage1(GROUP)

            def transposes1(i, k):
                n = i * 4 + k
                pe.wait_ge(n_in[1][k % AR], (i + (k // AR + 1)) * 32)
                transposed(bank[0], quarters(acc[:, k % AR, 0:D]), n, n_te0[1], n_t0[1])
                transposed(bank[1], quarters(acc[:, k % AR, D:2 * D]), n, n_te1[1], n_t1[1])

            def products1(n, k):
                pe.wait_ge(n_te0[1], after(n))
                pe.wait_ge(n_te1[1], after(n))
                pe.wait_ge(n_res[1], after(n - 2))
                for c in range(4):
                    s = slice(c * P, (c + 1) * P)
                    first, second = (2 * k, 2 * k + 1) if c == 0 else (2 * k + 1, 2 * k)
                    w = 0 if c == 0 else 2
                    nc.tensor.matmul(bank[2 + k][:, s], rows[:, first, s], wout_sb[:, w, :], start=True, stop=False)
                    last = nc.tensor.matmul(bank[2 + k][:, s], rows[:, second, s], wout_sb[:, w + 1, :],
                                            start=False, stop=True)
                last.then_inc(n_h[1], 1)

            def step1(i, c):
                if live(i, c + 2):
                    transposes1(i, c + 2)
                if live(i, c + 1):
                    products1(i * 4 + (c + 1), (c + 1) % 2)

            for k in range(2):
                transposes1(0, k)
            products1(0, 0)
            node_steps(pe, step1, 2, 0)


def kernel(**inputs):
    import numpy as np
    import concourse.bacc as bacc
    from concourse.bass_utils import run_bass_kernel_spmd

    def padded(a, rows, fill=0):
        return np.concatenate([a, np.full((rows - a.shape[0],) + a.shape[1:], fill, a.dtype)])

    def by_tile(a):
        return np.ascontiguousarray(a.reshape((-1, P) + a.shape[1:]).swapaxes(0, 1))

    a = {k: np.asarray(v) for k, v in inputs.items()}
    fill = np.full(1, N, a["dst"].dtype)
    dst = padded(a["dst"], T * P, N)
    feats = padded(a["edge_attr_8"], (NBLK + 2) * BLK * P).reshape(NBLK + 2, 2, BLK * P // 2, RB)
    arrays = {
        "x": padded(a["x"], NPAD),
        "src": by_tile(padded(a["src"], (T + 2 * BLK) * P)),
        "dst": by_tile(dst),
        "dst_before": by_tile(np.concatenate([fill, dst[:-1]])),
        "dst_after": by_tile(np.concatenate([dst[1:], fill])),
        "edge_y": by_tile(padded(a["edge_attr_4"], (T + BLK) * P)),
        "edge_feats": np.ascontiguousarray(feats.transpose(1, 3, 0, 2)).reshape(2 * RB, -1),
        "w_self": a["L0_gnn_W_self"],
        "b_self": a["L0_gnn_b_self"].reshape(1, D),
        "w_neigh": a["L0_gnn_W_neigh"],
        "gamma": a["L0_gnn_gamma"].reshape(1, D),
        "beta": a["L0_gnn_beta"].reshape(1, D),
        "alpha": a["L0_gnn_alpha"].reshape(1, 1),
    }
    for name in ("W_up0", "W_up1", "W_mlp1", "W_mlp2", "W_mlp3", "W_mlp4", "W_out0", "W_out1"):
        arrays[name.lower()] = a["L1_gnn_" + name]

    nc = bacc.Bacc("TRN2", target_bir_lowering=False, num_devices=1)
    args, dram = [], {}
    for name, value in arrays.items():
        dram[f"in_{name}"] = np.ascontiguousarray(value)
        args.append(nc.dram_tensor(f"in_{name}", value.shape, mybir.dt.from_np(value.dtype), kind="ExternalInput").ap())
    args.append(nc.dram_tensor("out_rows", [NT * P, D], fp32, kind="ExternalOutput").ap())
    build(nc, *args)
    r = run_bass_kernel_spmd(nc, [dram], core_ids=[0])
    return r.results[0]["out_rows"][:N]
```
